# Optimizing a Trainium2 kernel written in Bass

```python
import numpy as np
import jax
import jax.numpy as jnp

def _softmax(x, axis=-1):
    return jax.nn.softmax(x, axis=axis)

def _gelu(x):
    return jax.nn.gelu(x, approximate=True)

def _silu(x):
    return jax.nn.silu(x)

def _sigmoid(x):
    return jax.nn.sigmoid(x)

def _layernorm(x, axis=-1, eps=1e-05):
    m = jnp.mean(x, axis=axis, keepdims=True)
    v = jnp.var(x, axis=axis, keepdims=True)
    return (x - m) / jnp.sqrt(v + eps)

def _scatter_add(tgt, idx, src, axis=0):
    return tgt.at[idx].add(src)

def _segment_sum(src, seg, n):
    return jax.ops.segment_sum(src, seg, n)
kernel_name = 'mk_gnn_resnorm_d4_gnn_r16_633368'

def setup_inputs(seed: int=0):
    np.random.seed(seed)
    _w = jnp.asarray

    def _rec_inputs():
        import jax
        import jax.numpy as jnp
        _gk = jax.random.key(seed)
        x = -0.000364 + 1 * jax.random.normal(jax.random.fold_in(_gk, 1), (625, 768), jnp.float32)
        src = jax.random.randint(jax.random.fold_in(_gk, 2), (10000,), 0, 625, jnp.int32)
        dst = jnp.minimum((625 * jax.random.uniform(jax.random.fold_in(_gk, 3), (10000,)) ** 2.0).astype(jnp.int32), 9999)
        _o = jnp.argsort(dst, stable=True)
        src = src[_o]
        dst = dst[_o]
        edge_type_4 = jax.random.randint(jax.random.fold_in(_gk, 12), (10000,), 0, 4, jnp.int32)
        return (x, src, dst, edge_type_4)
    x, src, dst, edge_type_4 = _rec_inputs()

    def _L0_gnn_setup():
        import jax, jax.numpy as jnp
        import numpy as np
        N_NODES = 1250
        N_EDGES = 6250
        D = 768
        NUM_REL = 4

        def _rgcn_conv(x, weight, root, bias, src, dst, etype):
            n = x.shape[0]
            out = x @ root + bias
            for r in range(NUM_REL):
                sel = etype == r
                self_f = sel.astype(x.dtype)
                deg = jnp.zeros((n,), x.dtype).at[dst].add(self_f)
                norm = jnp.where(sel, 1.0 / jnp.maximum(deg[dst], 1.0), 0.0)
                h_r = x @ weight[r]
                msgs = h_r[src] * norm[:, None]
                out = out + jax.ops.segment_sum(msgs, dst, num_segments=n)
            return out
        key = jax.random.key(seed)
        ks = jax.random.split(key, 12)
        entity = jax.random.normal(ks[0], (N_NODES, D), dtype=jnp.float32)
        edge_index = jax.random.randint(ks[1], (2, N_EDGES), 0, N_NODES, dtype=jnp.int64)
        edge_type = jax.random.randint(ks[2], (N_EDGES,), 0, NUM_REL, dtype=jnp.int64)
        s = 0.02
        params = {}
        for i, layer in enumerate(['1', '2', '3']):
            params[f'W{layer}'] = jax.random.normal(ks[3 + 3 * i], (NUM_REL, D, D), dtype=jnp.float32) * s
            params[f'root{layer}'] = jax.random.normal(ks[4 + 3 * i], (D, D), dtype=jnp.float32) * s
            params[f'b{layer}'] = jnp.zeros((D,), dtype=jnp.float32)
        return {'entity': entity, 'edge_index': edge_index, 'edge_type': edge_type, **params}
    _L0_gnn_all = _L0_gnn_setup()
    _L0_gnn_in = {k: v for k, v in _L0_gnn_all.items() if k in ('W1', 'root1', 'b1', 'W2', 'root2', 'b2', 'W3', 'root3', 'b3')}
    del _L0_gnn_all

    def _L1_gnn_setup():
        import jax, jax.numpy as jnp
        import numpy as np
        N_NODES = 625
        D = 768
        N_EDGES = 10000

        def gcn_conv(x, W, b, src, dst, n_nodes):
            h = x @ W
            deg = jax.ops.segment_sum(jnp.ones_like(dst, dtype=h.dtype), dst, num_segments=n_nodes)
            dinv = jnp.where(deg > 0, jax.lax.rsqrt(deg), 0.0)
            norm = dinv[src] * dinv[dst]
            msgs = h[src] * norm[:, None]
            out = jax.ops.segment_sum(msgs, dst, num_segments=n_nodes)
            return out + b

        def add_self_loops(edge_index, n_nodes):
            loop = jnp.arange(n_nodes, dtype=edge_index.dtype)
            src = jnp.concatenate([edge_index[0], loop])
            dst = jnp.concatenate([edge_index[1], loop])
            return (src, dst)
        key = jax.random.key(seed)
        k1, k2, k3, k4 = jax.random.split(key, 4)
        x = jax.random.normal(k1, (N_NODES, D), dtype=jnp.float32)
        edge_index = jax.random.randint(k2, (2, N_EDGES), 0, N_NODES, dtype=jnp.int32)
        glorot = float(np.sqrt(6.0 / (D + D)))
        W1 = jax.random.uniform(k3, (D, D), jnp.float32, -glorot, glorot)
        W2 = jax.random.uniform(k4, (D, D), jnp.float32, -glorot, glorot)
        b1 = jnp.zeros((D,), jnp.float32)
        b2 = jnp.zeros((D,), jnp.float32)
        return {'x': x, 'W1': W1, 'b1': b1, 'W2': W2, 'b2': b2, 'edge_index': edge_index}
    _L1_gnn_all = _L1_gnn_setup()
    _L1_gnn_in = {k: v for k, v in _L1_gnn_all.items() if k in ('W1', 'b1', 'W2', 'b2')}
    del _L1_gnn_all

    def _L2_gnn_setup():
        import jax, jax.numpy as jnp
        import numpy as np
        N_NODES = 1250
        N_EDGES = 10000
        IN_DIM = 768
        HID = 256
        HEADS = 4
        OUT_DIM = 768
        LN_EPS = 1e-05

        def _add_self_loops(edge_index, n):
            loop = jnp.arange(n, dtype=edge_index.dtype)
            return jnp.concatenate([edge_index, jnp.stack([loop, loop])], axis=1)

        def gat_conv(x, edge_index, W, a_src, a_dst, bias, heads, out_ch, concat):
            n = x.shape[0]
            ei = _add_self_loops(edge_index, n)
            src, dst = (ei[0], ei[1])
            xl = (x @ W).reshape(n, heads, out_ch)
            alpha_src = jnp.einsum('nhc,hc->nh', xl, a_src)
            alpha_dst = jnp.einsum('nhc,hc->nh', xl, a_dst)
            e = jax.nn.leaky_relu(alpha_src[src] + alpha_dst[dst], 0.2)
            m = jax.ops.segment_max(e, dst, num_segments=n)
            e = jnp.exp(e - m[dst])
            s = jax.ops.segment_sum(e, dst, num_segments=n)
            alpha = e / (s[dst] + 1e-16)
            msg = xl[src] * alpha[:, :, None]
            out = jax.ops.segment_sum(msg, dst, num_segments=n)
            out = out.reshape(n, heads * out_ch) if concat else out.mean(axis=1)
            return out + bias

        def layer_norm(x, g, b):
            mu = jnp.mean(x, axis=-1, keepdims=True)
            var = jnp.var(x, axis=-1, keepdims=True)
            return (x - mu) * jax.lax.rsqrt(var + LN_EPS) * g + b
        key = jax.random.key(seed)
        ks = jax.random.split(key, 16)
        s = 0.02
        HC = HID * HEADS
        return {'x': jax.random.normal(ks[0], (N_NODES, IN_DIM), jnp.float32), 'edge_index': jax.random.randint(ks[1], (2, N_EDGES), 0, N_NODES, jnp.int64 if jax.config.jax_enable_x64 else jnp.int32), 'W1': jax.random.normal(ks[2], (IN_DIM, HC), jnp.float32) * s, 'a_src1': jax.random.normal(ks[3], (HEADS, HID), jnp.float32) * s, 'a_dst1': jax.random.normal(ks[4], (HEADS, HID), jnp.float32) * s, 'b1': jnp.zeros((HC,), jnp.float32), 'g1': jnp.ones((HC,), jnp.float32), 'be1': jnp.zeros((HC,), jnp.float32), 'Wr1': jax.random.normal(ks[5], (IN_DIM, HC), jnp.float32) * s, 'br1': jnp.zeros((HC,), jnp.float32), 'W2': jax.random.normal(ks[6], (HC, OUT_DIM), jnp.float32) * s, 'a_src2': jax.random.normal(ks[7], (1, OUT_DIM), jnp.float32) * s, 'a_dst2': jax.random.normal(ks[8], (1, OUT_DIM), jnp.float32) * s, 'b2': jnp.zeros((OUT_DIM,), jnp.float32), 'g2': jnp.ones((OUT_DIM,), jnp.float32), 'be2': jnp.zeros((OUT_DIM,), jnp.float32), 'Wr2': jax.random.normal(ks[9], (HC, OUT_DIM), jnp.float32) * s, 'br2': jnp.zeros((OUT_DIM,), jnp.float32)}
    _L2_gnn_all = _L2_gnn_setup()
    _L2_gnn_in = {k: v for k, v in _L2_gnn_all.items() if k in ('W1', 'a_src1', 'a_dst1', 'b1', 'g1', 'be1', 'Wr1', 'br1', 'W2', 'a_src2', 'a_dst2', 'b2', 'g2', 'be2', 'Wr2', 'br2')}
    del _L2_gnn_all

    def _L3_gnn_setup():
        import jax, jax.numpy as jnp
        import numpy as np
        N = 1250
        E_RAND = 20000
        NEG_SLOPE = 0.2

        def gat_layer(x, W, a_src, a_dst, bias, src, dst, heads, out_c, concat):
            n = x.shape[0]
            h = (x @ W).reshape(n, heads, out_c)
            al_s = jnp.einsum('nhc,hc->nh', h, a_src)
            al_d = jnp.einsum('nhc,hc->nh', h, a_dst)
            e = jax.nn.leaky_relu(al_s[src] + al_d[dst], NEG_SLOPE)
            m = jax.ops.segment_max(e, dst, num_segments=n)
            ex = jnp.exp(e - m[dst])
            z = jax.ops.segment_sum(ex, dst, num_segments=n)
            alpha = ex / (z[dst] + 1e-16)
            msg = h[src] * alpha[:, :, None]
            out = jax.ops.segment_sum(msg, dst, num_segments=n)
            out = out.reshape(n, heads * out_c) if concat else out.mean(axis=1)
            return out + bias
        key = jax.random.key(seed)
        ks = jax.random.split(key, 10)
        x = jax.random.normal(ks[0], (N, 768), dtype=jnp.float32)
        src = jax.random.randint(ks[1], (E_RAND,), 0, N)
        dst = jax.random.randint(ks[2], (E_RAND,), 0, N)
        loop = jnp.arange(N)
        edge_index = jnp.stack([jnp.concatenate([src, loop]), jnp.concatenate([dst, loop])])
        s = 1.0 / np.sqrt(768.0)
        W1 = jax.random.normal(ks[3], (768, 768), dtype=jnp.float32) * s
        a_src1 = jax.random.normal(ks[4], (8, 96), dtype=jnp.float32) * 0.1
        a_dst1 = jax.random.normal(ks[5], (8, 96), dtype=jnp.float32) * 0.1
        b1 = jnp.zeros((768,), dtype=jnp.float32)
        W2 = jax.random.normal(ks[6], (768, 768), dtype=jnp.float32) * s
        a_src2 = jax.random.normal(ks[7], (1, 768), dtype=jnp.float32) * 0.1
        a_dst2 = jax.random.normal(ks[8], (1, 768), dtype=jnp.float32) * 0.1
        b2 = jnp.zeros((768,), dtype=jnp.float32)
        return {'x': x, 'edge_index': edge_index, 'W1': W1, 'a_src1': a_src1, 'a_dst1': a_dst1, 'b1': b1, 'W2': W2, 'a_src2': a_src2, 'a_dst2': a_dst2, 'b2': b2}
    _L3_gnn_all = _L3_gnn_setup()
    _L3_gnn_in = {k: v for k, v in _L3_gnn_all.items() if k in ('W1', 'a_src1', 'a_dst1', 'b1', 'W2', 'a_src2', 'a_dst2', 'b2')}
    del _L3_gnn_all
    return {'x': x, 'src': src, 'dst': dst, 'edge_type_4': edge_type_4, 'L0_gnn_W1': _L0_gnn_in['W1'], 'L0_gnn_root1': _L0_gnn_in['root1'], 'L0_gnn_b1': _L0_gnn_in['b1'], 'L0_gnn_W2': _L0_gnn_in['W2'], 'L0_gnn_root2': _L0_gnn_in['root2'], 'L0_gnn_b2': _L0_gnn_in['b2'], 'L0_gnn_W3': _L0_gnn_in['W3'], 'L0_gnn_root3': _L0_gnn_in['root3'], 'L0_gnn_b3': _L0_gnn_in['b3'], 'L1_gnn_W1': _L1_gnn_in['W1'], 'L1_gnn_b1': _L1_gnn_in['b1'], 'L1_gnn_W2': _L1_gnn_in['W2'], 'L1_gnn_b2': _L1_gnn_in['b2'], 'L2_gnn_W1': _L2_gnn_in['W1'], 'L2_gnn_a_src1': _L2_gnn_in['a_src1'], 'L2_gnn_a_dst1': _L2_gnn_in['a_dst1'], 'L2_gnn_b1': _L2_gnn_in['b1'], 'L2_gnn_g1': _L2_gnn_in['g1'], 'L2_gnn_be1': _L2_gnn_in['be1'], 'L2_gnn_Wr1': _L2_gnn_in['Wr1'], 'L2_gnn_br1': _L2_gnn_in['br1'], 'L2_gnn_W2': _L2_gnn_in['W2'], 'L2_gnn_a_src2': _L2_gnn_in['a_src2'], 'L2_gnn_a_dst2': _L2_gnn_in['a_dst2'], 'L2_gnn_b2': _L2_gnn_in['b2'], 'L2_gnn_g2': _L2_gnn_in['g2'], 'L2_gnn_be2': _L2_gnn_in['be2'], 'L2_gnn_Wr2': _L2_gnn_in['Wr2'], 'L2_gnn_br2': _L2_gnn_in['br2'], 'L3_gnn_W1': _L3_gnn_in['W1'], 'L3_gnn_a_src1': _L3_gnn_in['a_src1'], 'L3_gnn_a_dst1': _L3_gnn_in['a_dst1'], 'L3_gnn_b1': _L3_gnn_in['b1'], 'L3_gnn_W2': _L3_gnn_in['W2'], 'L3_gnn_a_src2': _L3_gnn_in['a_src2'], 'L3_gnn_a_dst2': _L3_gnn_in['a_dst2'], 'L3_gnn_b2': _L3_gnn_in['b2']}

def reference(x, src, dst, edge_type_4, L0_gnn_W1, L0_gnn_root1, L0_gnn_b1, L0_gnn_W2, L0_gnn_root2, L0_gnn_b2, L0_gnn_W3, L0_gnn_root3, L0_gnn_b3, L1_gnn_W1, L1_gnn_b1, L1_gnn_W2, L1_gnn_b2, L2_gnn_W1, L2_gnn_a_src1, L2_gnn_a_dst1, L2_gnn_b1, L2_gnn_g1, L2_gnn_be1, L2_gnn_Wr1, L2_gnn_br1, L2_gnn_W2, L2_gnn_a_src2, L2_gnn_a_dst2, L2_gnn_b2, L2_gnn_g2, L2_gnn_be2, L2_gnn_Wr2, L2_gnn_br2, L3_gnn_W1, L3_gnn_a_src1, L3_gnn_a_dst1, L3_gnn_b1, L3_gnn_W2, L3_gnn_a_src2, L3_gnn_a_dst2, L3_gnn_b2):
    import jax
    import jax.numpy as jnp

    def _L0_gnn_ref(entity, edge_index, edge_type, W1, root1, b1, W2, root2, b2, W3, root3, b3):
        import jax, jax.numpy as jnp
        import numpy as np
        N_NODES = 1250
        N_EDGES = 6250
        D = 768
        NUM_REL = 4

        def _rgcn_conv(x, weight, root, bias, src, dst, etype):
            n = x.shape[0]
            out = x @ root + bias
            for r in range(NUM_REL):
                sel = etype == r
                self_f = sel.astype(x.dtype)
                deg = jnp.zeros((n,), x.dtype).at[dst].add(self_f)
                norm = jnp.where(sel, 1.0 / jnp.maximum(deg[dst], 1.0), 0.0)
                h_r = x @ weight[r]
                msgs = h_r[src] * norm[:, None]
                out = out + jax.ops.segment_sum(msgs, dst, num_segments=n)
            return out
        src, dst = (edge_index[0], edge_index[1])
        x = jax.nn.relu(_rgcn_conv(entity, W1, root1, b1, src, dst, edge_type))
        x = jax.nn.relu(_rgcn_conv(x, W2, root2, b2, src, dst, edge_type))
        x = _rgcn_conv(x, W3, root3, b3, src, dst, edge_type)
        return x

    def _L1_gnn_ref(x, W1, b1, W2, b2, edge_index):
        import jax, jax.numpy as jnp
        import numpy as np
        N_NODES = 625
        D = 768
        N_EDGES = 10000

        def gcn_conv(x, W, b, src, dst, n_nodes):
            h = x @ W
            deg = jax.ops.segment_sum(jnp.ones_like(dst, dtype=h.dtype), dst, num_segments=n_nodes)
            dinv = jnp.where(deg > 0, jax.lax.rsqrt(deg), 0.0)
            norm = dinv[src] * dinv[dst]
            msgs = h[src] * norm[:, None]
            out = jax.ops.segment_sum(msgs, dst, num_segments=n_nodes)
            return out + b

        def add_self_loops(edge_index, n_nodes):
            loop = jnp.arange(n_nodes, dtype=edge_index.dtype)
            src = jnp.concatenate([edge_index[0], loop])
            dst = jnp.concatenate([edge_index[1], loop])
            return (src, dst)
        n = x.shape[0]
        src, dst = add_self_loops(edge_index, n)
        h = gcn_conv(x, W1, b1, src, dst, n)
        h = jax.nn.relu(h)
        out = gcn_conv(h, W2, b2, src, dst, n)
        return out

    def _L2_gnn_ref(x, edge_index, W1, a_src1, a_dst1, b1, g1, be1, Wr1, br1, W2, a_src2, a_dst2, b2, g2, be2, Wr2, br2):
        import jax, jax.numpy as jnp
        import numpy as np
        N_NODES = 1250
        N_EDGES = 10000
        IN_DIM = 768
        HID = 256
        HEADS = 4
        OUT_DIM = 768
        LN_EPS = 1e-05

        def _add_self_loops(edge_index, n):
            loop = jnp.arange(n, dtype=edge_index.dtype)
            return jnp.concatenate([edge_index, jnp.stack([loop, loop])], axis=1)

        def gat_conv(x, edge_index, W, a_src, a_dst, bias, heads, out_ch, concat):
            n = x.shape[0]
            ei = _add_self_loops(edge_index, n)
            src, dst = (ei[0], ei[1])
            xl = (x @ W).reshape(n, heads, out_ch)
            alpha_src = jnp.einsum('nhc,hc->nh', xl, a_src)
            alpha_dst = jnp.einsum('nhc,hc->nh', xl, a_dst)
            e = jax.nn.leaky_relu(alpha_src[src] + alpha_dst[dst], 0.2)
            m = jax.ops.segment_max(e, dst, num_segments=n)
            e = jnp.exp(e - m[dst])
            s = jax.ops.segment_sum(e, dst, num_segments=n)
            alpha = e / (s[dst] + 1e-16)
            msg = xl[src] * alpha[:, :, None]
            out = jax.ops.segment_sum(msg, dst, num_segments=n)
            out = out.reshape(n, heads * out_ch) if concat else out.mean(axis=1)
            return out + bias

        def layer_norm(x, g, b):
            mu = jnp.mean(x, axis=-1, keepdims=True)
            var = jnp.var(x, axis=-1, keepdims=True)
            return (x - mu) * jax.lax.rsqrt(var + LN_EPS) * g + b
        h0 = x
        h = gat_conv(x, edge_index, W1, a_src1, a_dst1, b1, HEADS, HID, True)
        h = layer_norm(h, g1, be1)
        h = jax.nn.relu(h)
        h = h + (h0 @ Wr1 + br1)
        h1 = h
        h = gat_conv(h, edge_index, W2, a_src2, a_dst2, b2, 1, OUT_DIM, False)
        h = layer_norm(h, g2, be2)
        h = h + (h1 @ Wr2 + br2)
        return h

    def _L3_gnn_ref(x, edge_index, W1, a_src1, a_dst1, b1, W2, a_src2, a_dst2, b2):
        import jax, jax.numpy as jnp
        import numpy as np
        N = 1250
        E_RAND = 20000
        NEG_SLOPE = 0.2

        def gat_layer(x, W, a_src, a_dst, bias, src, dst, heads, out_c, concat):
            n = x.shape[0]
            h = (x @ W).reshape(n, heads, out_c)
            al_s = jnp.einsum('nhc,hc->nh', h, a_src)
            al_d = jnp.einsum('nhc,hc->nh', h, a_dst)
            e = jax.nn.leaky_relu(al_s[src] + al_d[dst], NEG_SLOPE)
            m = jax.ops.segment_max(e, dst, num_segments=n)
            ex = jnp.exp(e - m[dst])
            z = jax.ops.segment_sum(ex, dst, num_segments=n)
            alpha = ex / (z[dst] + 1e-16)
            msg = h[src] * alpha[:, :, None]
            out = jax.ops.segment_sum(msg, dst, num_segments=n)
            out = out.reshape(n, heads * out_c) if concat else out.mean(axis=1)
            return out + bias
        src, dst = (edge_index[0], edge_index[1])
        h = gat_layer(x, W1, a_src1, a_dst1, b1, src, dst, heads=8, out_c=96, concat=True)
        h = jax.nn.elu(h)
        out = gat_layer(h, W2, a_src2, a_dst2, b2, src, dst, heads=1, out_c=768, concat=False)
        return out
    edge_index = jnp.stack([src, dst])
    x = _layernorm(x + _L0_gnn_ref(x, edge_index, edge_type_4, L0_gnn_W1, L0_gnn_root1, L0_gnn_b1, L0_gnn_W2, L0_gnn_root2, L0_gnn_b2, L0_gnn_W3, L0_gnn_root3, L0_gnn_b3), axis=-1)
    x = _layernorm(x + _L1_gnn_ref(x, L1_gnn_W1, L1_gnn_b1, L1_gnn_W2, L1_gnn_b2, edge_index), axis=-1)
    x = _layernorm(x + _L2_gnn_ref(x, edge_index, L2_gnn_W1, L2_gnn_a_src1, L2_gnn_a_dst1, L2_gnn_b1, L2_gnn_g1, L2_gnn_be1, L2_gnn_Wr1, L2_gnn_br1, L2_gnn_W2, L2_gnn_a_src2, L2_gnn_a_dst2, L2_gnn_b2, L2_gnn_g2, L2_gnn_be2, L2_gnn_Wr2, L2_gnn_br2), axis=-1)
    x = _layernorm(x + _L3_gnn_ref(x, edge_index, L3_gnn_W1, L3_gnn_a_src1, L3_gnn_a_dst1, L3_gnn_b1, L3_gnn_W2, L3_gnn_a_src2, L3_gnn_a_dst2, L3_gnn_b2), axis=-1)
    return x

_drawn_inputs = setup_inputs


def setup_inputs(seed=0):
    import zlib

    import numpy as np

    out = dict(_drawn_inputs(seed))
    spreads = {'L0_gnn_b1': (0.0, 0.1),
     'L0_gnn_b2': (0.0, 0.1),
     'L0_gnn_b3': (0.0, 0.1),
     'L1_gnn_b1': (0.0, 0.1),
     'L1_gnn_b2': (0.0, 0.1),
     'L2_gnn_b1': (0.0, 0.1),
     'L2_gnn_g1': (1.0, 0.2),
     'L2_gnn_be1': (0.0, 0.1),
     'L2_gnn_br1': (0.0, 0.1),
     'L2_gnn_b2': (0.0, 0.1),
     'L2_gnn_g2': (1.0, 0.2),
     'L2_gnn_be2': (0.0, 0.1),
     'L2_gnn_br2': (0.0, 0.1),
     'L3_gnn_b1': (0.0, 0.1),
     'L3_gnn_b2': (0.0, 0.1)}
    factors = {'L2_gnn_a_src1': 3.371,
     'L2_gnn_a_dst1': 8.0,
     'L2_gnn_a_src2': 5.998,
     'L2_gnn_a_dst2': 8.0,
     'L3_gnn_a_dst1': 7.52,
     'L3_gnn_a_dst2': 8.0}
    for name, (base, spread) in spreads.items():
        noise = np.random.default_rng([zlib.crc32(name.encode()), seed]).standard_normal(out[name].shape)
        drawn = base * np.exp(spread * noise) if base else spread * noise
        out[name] = jnp.asarray(drawn.astype(out[name].dtype))
    for name, factor in factors.items():
        out[name] = (out[name] * factor).astype(out[name].dtype)
    return out
```

```python
from contextlib import ExitStack

import concourse.bass as bass
from concourse import mybir

F32 = mybir.dt.float32
F32R = mybir.dt.float32r
BF16 = mybir.dt.bfloat16
FP16 = mybir.dt.float16
I32 = mybir.dt.int32
I16 = mybir.dt.int16
ALU = mybir.AluOpType
ACT = mybir.ActivationFunctionType

N = 625
D = 768
E = 10000
BP = 125
NB = N // BP
KC = D // 128
HW = 384
NREL = 4
RLAYERS = 3
PAIR_BASE = 4096
ET = E // BP
SWEEP = 27
CHUNKS = -(-ET // SWEEP)
ETP = SWEEP * CHUNKS
HID = 1024
HEADS2, C2 = 4, 256
HEADS3, C3 = 8, 96
WRING = 10
OH_RING = 3
RAW = 5
NEG = -1.0e30
LN_EPS = 1e-5
SLOPE = 0.2

L0_CHUNKS = 2 * KC * (NREL + 1)
PIECES1 = [(0, 384), (384, 384), (768, 256)]
PIECES = [(0, 384), (384, 384)]
K8 = HID // 128


def gemm_chunks(k, pieces):
    return k * len(pieces)


BASE_L1 = RLAYERS * L0_CHUNKS
BASE_L2 = BASE_L1 + 2 * gemm_chunks(KC, PIECES)
BASE_L2B = BASE_L2 + 2 * gemm_chunks(KC, PIECES1)
BASE_L3 = BASE_L2B + 2 * gemm_chunks(K8, PIECES)
NCHUNKS = BASE_L3 + 2 * gemm_chunks(KC, PIECES)


class Attention:

    def __init__(self, before, heads, c, k, pieces, residual, chunk, loops):
        self.heads, self.c, self.k, self.pieces, self.residual, self.chunk = heads, c, k, pieces, residual, chunk
        self.index = before.index + 1 if before else 0
        self.loops = loops
        self.w = c + 1
        self.parts = ([(h, h * self.w, self.w) for h in range(heads)] if heads > 1
                      else [(0, HW, HW + 1), (0, 0, HW)])
        self.ring = 3 if heads > 1 else 5
        self.blocks = NB * len(pieces)
        g = before
        self.gemm0 = g.gemm0 + g.blocks * (1 + g.residual) if g else 0
        self.head0 = g.head0 + g.heads if g else 0
        self.part0 = g.part0 + len(g.parts) if g else 0
        n = NB * len(pieces) if residual else 0
        self.fill = [5] + [3] * (heads - 1) if residual else [0] * heads
        self.fill.append(n - sum(self.fill))


Q0 = Attention(None, HEADS2, C2, KC, PIECES1, True, BASE_L2, True)
Q1 = Attention(Q0, 1, D, K8, PIECES, True, BASE_L2B, True)
Q2 = Attention(Q1, HEADS3, C3, KC, PIECES, False, BASE_L3, False)
Q3 = Attention(Q2, 1, D, KC, PIECES, False, BASE_L3 + 2 * KC, False)


class Memory:

    def __init__(self, nc):
        base = (nc.sbuf_base + 63) // 64 * 64

        def at(name, shape, dt, offset):
            return nc.alloc_sbuf_tensor_at(name, shape, dt, offset=base + offset)

        self.ident = at("ident", [128, 128], F32, 0)
        self.ones = at("ones", [128, 16], F32, 512)
        small = 576
        wh = 2688
        wl = wh + WRING * HW * 4
        raw = wl + WRING * HW * 4
        x = raw + RAW * HW * 4
        xn = x + 30016
        ah = xn + D * NB * 4
        al = ah + 50016
        ci = al + 50016
        h = ci + 6272
        bias = h + 6144
        tail = bias + 9216
        assert base + tail + 4096 <= nc.sbuf_usable_end

        self.wh = at("w_hi", [128, WRING, HW], F32R, wh)
        self.wl = at("w_lo", [128, WRING, HW], F32R, wl)
        self.raw = at("w_raw", [128, RAW, HW], F32, raw)
        self.xh = at("xT_hi", [128, KC, N], F32R, x)
        self.xl = at("xT_lo", [128, KC, N], F32R, x + 15008)
        self.xn = at("x_nat", [128, NB, D], F32, xn)
        self.ah = at("adj_hi", [128, NREL, NB, N], F32R, ah)
        self.al = at("adj_lo", [128, NREL, NB, N], F32R, al)
        self.cnt = at("edge_counts", [128, NREL, NB, N], F32, al)
        self.ctot = at("counts_all", [128, NB, N], I16, ci)
        self.hh = at("h_hi", [128, 2, HW], F32R, h)
        self.hl = at("h_lo", [128, 2, HW], F32R, h + 2 * HW * 4)
        self.bias0 = at("rgcn_bias", [128, RLAYERS, D], F32, bias)

        self.sweep = at("sweep_sums", [128, 2, NB, N], I32, ah)
        self.odd = at("sweep_odd", [128, 2, N], I32, ah + 25024)
        self.oh_src = at("onehot_src", [128, OH_RING, N], BF16, ah + 30080)
        self.oh_dst = at("onehot_dst", [128, OH_RING, N], BF16, ah + 35136)
        self.iota = at("iota", [128, N], FP16, ah + 40192)
        edges = ah + 41472
        self.edges_i = at("edges_int", [128, 3, ET], I32, edges)
        self.src_f = at("src_f", [128, ETP], F32, edges + 960)
        self.dst_f = at("dst_f", [128, ETP], F32, edges + 1312)
        self.typ_f = at("typ_f", [128, ETP], F32, edges + 1664)
        self.val_f = at("val_f", [128, ETP], F32, edges + 2016)
        self.tmp_f = at("tmp_f", [128, ETP], F32, edges + 2368)
        self.dstp_f = at("dst_of_pair", [128, 2, ETP], F32, edges + 2720)
        self.inv = at("inv_degree", [128, NREL, N], F32, ah + 37504 + 2016)

        self.stats = at("ln_stats", [128, NB, 2, 6], F32, small)
        self.mv = at("ln_mean_var", [128, NB, 2], F32, small + 256)
        self.std = at("ln_std", [128, NB], F32, small + 320)
        self.dinv = at("gcn_dinv", [128, NB], F32, small + 384)
        self.deg = at("gcn_deg", [128, NB], F32, small + 448)
        self.xres = at("x_residual", [128, NB, D], F32, ah)
        self.ch = at("gcn_counts_hi", [128, NB, N], F32R, ah + 15360)
        self.cl = at("gcn_counts_lo", [128, NB, N], F32R, ah + 27904)
        self.cf = at("gcn_counts", [128, NB, N], F32, ah + 56416)
        self.bias1 = at("gcn_bias", [128, 2, D], F32, bias)
        self.diag = at("mask_diagonal", [128, BP], F32, ah + 68928)

        self.feat = at("features", [128, 1028 * NB], F32, ah + 15360)
        self.resid = at("residual_product", [128, NB, HID], F32, ah + 35936)
        self.prob = at("probs", [128, 5, N], F32, ah + 56416)
        self.score = at("scores", [128, 3, N], F32, ah + 68928)
        self.rows = at("score_rows", [128, 2, 2 * N], F32, ah + 76448)
        self.mask_loop = at("mask_loops", [128, NB, N], BF16, ah + 86464)
        self.mask_plain = at("mask_plain", [128, NB, N], BF16, ah + 92736)
        self.cnt_loop = at("counts_loops", [128, NB, N], I16, bias)
        self.par = [at("par0", [128, HID], F32, h), at("par1", [128, HID], F32, tail),
                    at("par2", [128, HID], F32, ah + 56416 + 7520), at("par3", [128, HID], F32, x + 40000)]
        self.par0b = at("par0b", [128, D], F32, h + 3072)
        self.xh8 = at("x8T_hi", [128, K8, N], F32R, x)
        self.xl8 = at("x8T_lo", [128, K8, N], F32R, x + 20000)
        cols = small + 512
        (self.al_src, self.al_dst, self.al_src2, self.al_max, self.row1, self.row2, self.al_sum) = (
            at(n, [128, NB, HEADS3], F32, cols + 160 * i) for i, n in enumerate(
                ("al_src", "al_dst", "al_src_slope", "al_max", "row_steep", "row_flat", "al_sum")))
        self.z = at("z", [128, NB], F32, cols + 160 * 7)


def program(nc, x, src, dst, etype, weights, rgcn_bias, gcn_bias, vec, out):
    ctx = ExitStack()
    with ctx:
        nc.disable_value_cache = True
        mem = Memory(nc)
        ps = ctx.enter_context(nc.psum_tensor("psum", [128, 8 * 512], F32))

        def sem(name):
            return ctx.enter_context(nc.semaphore(name))

        consts_ready = sem("consts_ready")
        edges_loaded = sem("edges_loaded")
        x_loaded = sem("x_loaded")
        bias_loaded = sem("bias_loaded")
        edges_ready = sem("edges_ready")
        onehot_ready = sem("onehot_ready")
        onehot_used = sem("onehot_used")
        sweep_done = sem("sweep_done")
        sweep_read = sem("sweep_read")
        decoded = sem("decoded")
        degree_done = sem("degree_done")
        inv_ready = sem("inv_ready")
        adj_scaled = sem("adj_scaled")
        adj_hi_ready = sem("adj_hi_ready")
        adj_lo_ready = sem("adj_lo_ready")
        raw_loaded = [sem(f"raw_loaded{i}") for i in range(RAW)]
        w_hi_ready = sem("w_hi_ready")
        w_lo_ready = sem("w_lo_ready")
        w_used = sem("w_used")
        pool_turn = sem("pool_turn")
        turned = sem("turned")
        xT_hi_ready = sem("xT_hi_ready")
        xT_lo_ready = sem("xT_lo_ready")
        h_done = sem("h_done")
        h_hi_ready = sem("h_hi_ready")
        h_lo_ready = sem("h_lo_ready")
        agg_used = sem("agg_used")
        out_done = sem("out_done")
        out_read = sem("out_read")
        vchain = sem("vchain")
        res_loaded = sem("res_loaded")
        stored = sem("stored")
        var_ready = sem("var_ready")
        std_ready = sem("std_ready")
        normed = sem("normed")
        gcn_ready = sem("gcn_ready")
        gdeg_done = sem("gdeg_done")
        gdeg_ready = sem("gdeg_ready")
        gsqrt_ready = sem("gsqrt_ready")
        dinv_ready = sem("dinv_ready")

        UNITS = len(range(KC)) + 2
        T_L1 = UNITS * (1 + RLAYERS)
        H_LAYER = 2 * NREL * NB
        H_L1 = RLAYERS * H_LAYER
        TAIL = N - 512
        SWEEP_BANKS = [(5, 512, N), (6, 512, N)] + [(m, 0, 512) for m in range(NB)]
        XRES_AT, BIAS1_AT = 175, 190

        def bank(b, a=0, e=512, p=BP):
            return ps[0:p, b * 512 + a:b * 512 + e]

        def rows(t, m, a, e):
            return t[0:BP, m, a:e]

        def nodes(m):
            return slice(m * BP, (m + 1) * BP)

        def turn_units(k):
            units = [[(c, m) for m in range(4)] for c in range(k)]
            return units + [[(c, 4) for c in range(j, min(j + 4, k))] for j in range(0, k, 4)]

        def unit_out(t, unit):
            (c0, m0), n = unit[0], len(unit)
            if m0 == 0:
                return t[:, c0, 0:4 * BP]
            return t[:, c0:c0 + n, 4 * BP:N]

        def unit_in(b, unit):
            n = len(unit)
            v = ps[:, b * 512:b * 512 + n * BP]
            return v if unit[0][1] == 0 else v.rearrange("p (c n) -> p c n", c=n)

        block = ctx.enter_context(nc.Block())

        gemm_done = sem("gemm_done")
        gemm_read = sem("gemm_read")
        params_loaded = sem("params_loaded")
        al_ready = sem("al_ready")
        max_row_done = sem("max_row_done")
        max_done = sem("max_done")
        cols_ready = sem("cols_ready")
        rows_done = sem("rows_done")
        rows_read = sem("rows_read")
        arg_ready = sem("arg_ready")
        exp_done = sem("exp_done")
        prob_ready = sem("prob_ready")
        prob_used = sem("prob_used")
        part_done = sem("part_done")
        part_read = sem("part_read")
        bias_added = sem("bias_added")
        mask_done = sem("mask_done")
        mask_read = sem("mask_read")
        layer_ready = sem("layer_ready")
        elu_in = sem("elu_in")
        elu_out = sem("elu_out")

        T_Q = [T_L1 + 2 * UNITS]
        T_Q += [T_Q[0] + UNITS, T_Q[0] + UNITS + K8 + 2]
        T_Q += [T_Q[2] + UNITS]

        def score_pieces(off):
            for m in range(NB):
                a, e = off + m * BP, off + (m + 1) * BP
                cut = -(-(a + 1) // 512) * 512
                for p, q in ((a, min(e, cut)), (cut, e)):
                    if q > p:
                        yield m, p, q, p - a, q - a

        def feat(q, m, h0=0, h1=None):
            v = mem.feat[0:BP, 0:NB * q.heads * q.w].rearrange("p (m h w) -> p m h w", m=NB, h=q.heads)
            return v[:, m, h0:q.heads if h1 is None else h1, 0:q.c]

        def feat_flat(q, m, a, e):
            v = mem.feat[0:BP, 0:NB * q.heads * q.w].rearrange("p (m n) -> p m n", m=NB)
            return v[:, m, a:e]

        def features_of(q, piece):
            a, width = piece
            h, out = a // q.c, []
            while h * q.c < a + width:
                p, e = max(a, h * q.c), min(a + width, (h + 1) * q.c)
                out.append((h, p - h * q.c, e - h * q.c, p - a))
                h += 1
            return out

        def gemm_bank(q, g):
            return 5 + g % 3

        @block.sync
        def _(sp):
            for i, v in enumerate((src, dst, etype)):
                sp.dma_start(mem.edges_i[0:BP, i, :], v.rearrange("(p t) -> p t", t=ET)).then_inc(edges_loaded, 16)
            sp.dma_start(mem.xn[0:BP, :, :], x.rearrange("(m p) d -> p m d", p=BP)).then_inc(x_loaded, 16)
            sp.dma_start(mem.bias0[0:BP, :, :].rearrange("p l d -> p (l d)"),
                         rgcn_bias.rearrange("(a l) d -> a (l d)", a=1).to_broadcast([BP, RLAYERS * D])
                         ).then_inc(bias_loaded, 16)

            def load(c, slot, first=False):
                if not first:
                    sp.wait_ge(w_lo_ready, c - RAW + 1)
                sp.dma_start(mem.raw[:, slot, :], weights[bass.ds(c, 1), :, :].rearrange("a p n -> p (a n)")
                             ).then_inc(raw_loaded[slot], 16)

            for c in range(RAW):
                load(c, c, first=True)
            with sp.Fori(1, XRES_AT // RAW) as i:
                for slot in range(RAW):
                    load(i * RAW + slot, slot)
            sp.wait_ge(agg_used, (2 * RLAYERS - 1) * (NREL * NB - 1) + 2 * NB)
            sp.dma_start(mem.xres[0:BP, :, :], x.rearrange("(m p) d -> p m d", p=BP)).then_inc(res_loaded, 16)
            with sp.Fori(XRES_AT // RAW, BIAS1_AT // RAW) as i:
                for slot in range(RAW):
                    load(i * RAW + slot, slot)
            sp.wait_ge(out_read, 10 * RLAYERS)
            sp.dma_start(mem.bias1[0:BP, :, :].rearrange("p l d -> p (l d)"),
                         gcn_bias.rearrange("(a l) d -> a (l d)", a=1).to_broadcast([BP, 2 * D])
                         ).then_inc(bias_loaded, 16)
            with sp.Fori(BIAS1_AT // RAW, NCHUNKS // RAW) as i:
                for slot in range(RAW):
                    load(i * RAW + slot, slot)
            for c in range(NCHUNKS // RAW * RAW, NCHUNKS):
                load(c, c % RAW)
            o = out.rearrange("(m p) d -> p m d", p=BP)
            for m in range(NB):
                sp.wait_ge(normed, 3 * NB + m + 1)
                sp.dma_start(o[:, m, :], mem.xres[0:BP, m, :]).then_inc(stored, 16)
            sp.wait_ge(stored, 16 * NB)

        @block.gpsimd
        def _(pool):
            nc.gpsimd.memset(mem.ones[:, :], 1.0)
            nc.gpsimd.iota(mem.iota[:, :], pattern=[[1, N]], base=0, channel_multiplier=0,
                           allow_small_or_imprecise_dtypes=True)
            nc.gpsimd.memset(mem.ident[:, :], 0.0).then_inc(consts_ready, 1)
            pool.wait_ge(consts_ready, 1)
            nc.gpsimd.affine_select(out=mem.ident[:, :], in_=mem.ident[:, :], compare_op=ALU.not_equal, fill=1.0,
                                    base=0, pattern=[[-1, 128]], channel_multiplier=1).then_inc(consts_ready, 1)

            def split(c, slot, raw_slot, turn, first=False):
                if not first:
                    pool.wait_ge(w_used, c - WRING + 1)
                pool.wait_ge(raw_loaded[raw_slot], 16 * turn)
                pool.sem_inc(pool_turn, 1)
                nc.gpsimd.tensor_copy(mem.wh[:, slot, :], mem.raw[:, raw_slot, :]).then_inc(w_hi_ready, 1)
                pool.wait_ge(w_hi_ready, c + 1)
                nc.gpsimd.tensor_tensor(mem.wl[:, slot, :], mem.raw[:, raw_slot, :],
                                        mem.wh[:, slot, :].bitcast(F32), ALU.subtract).then_inc(w_lo_ready, 1)

            for c in range(WRING):
                split(c, c, c % RAW, c // RAW + 1, first=True)
            def split_loop(c0, c1):
                with pool.Fori(c0 // WRING, c1 // WRING) as i:
                    for j in range(WRING):
                        split(i * WRING + j, j, j % RAW, i * (WRING // RAW) + j // RAW + 1)

            at1, at2 = BASE_L2B // WRING * WRING + WRING, BASE_L3 // WRING * WRING + WRING
            split_loop(WRING, at1)
            pool.wait_ge(gemm_read, Q0.gemm0 + 2 * Q0.blocks)
            pool.wait_ge(params_loaded, 16 * 4)
            for m in range(NB):
                r = mem.resid[0:BP, m, :]
                nc.gpsimd.tensor_tensor(r, r, mem.par[3][0:BP, :], ALU.add).then_inc(bias_added, 1)
            split_loop(at1, at2)
            pool.wait_ge(gemm_read, Q1.gemm0 + 2 * Q1.blocks)
            pool.wait_ge(params_loaded, 16 * (6 + 4))
            for m in range(NB):
                r = mem.resid[0:BP, m, 0:D]
                nc.gpsimd.tensor_tensor(r, r, mem.par[3][0:BP, 0:D], ALU.add).then_inc(bias_added, 1)
                pool.wait_ge(bias_added, NB + 2 * m + 1)
                nc.gpsimd.tensor_tensor(r, r, mem.xres[0:BP, m, :], ALU.add).then_inc(bias_added, 1)
            split_loop(at2, NCHUNKS)
            for c in range(NCHUNKS // WRING * WRING, NCHUNKS):
                split(c, c % WRING, c % RAW, c // RAW + 1)

        @block.scalar
        def _(act):
            def turn_hi(u0, k, dst_hi, func):
                for u, unit in enumerate(turn_units(k)):
                    act.wait_ge(turned, u0 + u + 1)
                    nc.scalar.activation(unit_out(dst_hi, unit), unit_in(u % 8, unit), func).then_inc(xT_hi_ready, 1)

            def read_sweep(done, free, s):
                for j, (b, a, e) in enumerate(SWEEP_BANKS):
                    act.wait_ge(sweep_done, done + j + 1)
                    if j == 0:
                        act.wait_ge(decoded, free + 1)
                    if b == 5:
                        o, i = mem.sweep[0:BP, s, 0:4, 512:N], bank(5, 0, 4 * TAIL).rearrange("p (m n) -> p m n", m=4)
                    elif b == 6:
                        o, i = mem.sweep[0:BP, s, 4, 512:N], bank(6, 0, TAIL)
                    else:
                        o, i = mem.sweep[0:BP, s, b, 0:512], bank(b)
                    nc.scalar.activation(o, i, ACT.Copy).then_inc(sweep_read, 1)

            def h_hi(i, slot, scale=None):
                act.wait_ge(h_done, i + 1)
                if scale is None:
                    nc.scalar.activation(mem.hh[0:BP, slot, :], bank(5 + slot, 0, HW), ACT.Copy
                                         ).then_inc(h_hi_ready, 1)
                else:
                    nc.scalar.activation(mem.hh[0:BP, slot, :], bank(5 + slot, 0, HW), ACT.Copy, scale=scale
                                         ).then_inc(h_hi_ready, 1)

            turn_hi(0, KC, mem.xh, ACT.Copy)
            act.sem_inc(sweep_read, 1)
            with act.Fori(0, CHUNKS) as c:
                read_sweep(c * 14, c * 40, 0)
                read_sweep(c * 14 + 7, c * 40 + 20, 1)
            for r in range(NREL):
                act.wait_ge(adj_scaled, r + 1)
                nc.scalar.activation(mem.ah[0:BP, r, :, :], mem.cnt[0:BP, r, :, :], ACT.Copy).then_inc(adj_hi_ready, 1)
            with act.Fori(0, RLAYERS) as l:
                for i in range(H_LAYER):
                    h_hi(l * H_LAYER + i, i % 2)
                turn_hi(l * UNITS + UNITS, KC, mem.xh, ACT.Relu)

            def layer_std(n):
                act.wait_ge(var_ready, n + 1)
                nc.scalar.activation(mem.std[0:BP, :], mem.std[0:BP, :], ACT.Sqrt).then_inc(std_ready, 1)

            layer_std(0)
            turn_hi(T_L1, KC, mem.xh, ACT.Copy)
            act.wait_ge(gcn_ready, 1)
            nc.scalar.activation(mem.ch[0:BP, :, :], mem.cf[0:BP, :, :], ACT.Copy).then_inc(gcn_ready, 1)
            act.wait_ge(gdeg_ready, 1)
            nc.scalar.activation(mem.deg[0:BP, :], mem.deg[0:BP, :], ACT.Sqrt).then_inc(gsqrt_ready, 1)
            act.wait_ge(dinv_ready, 1)
            for layer in range(2):
                for i in range(2 * NB):
                    h_hi(H_L1 + layer * 2 * NB + i, i % 2, mem.dinv[0:BP, i % NB:i % NB + 1])
                if layer == 0:
                    turn_hi(T_L1 + UNITS, KC, mem.xh, ACT.Relu)
            layer_std(1)

            def load_row(name, row, width):
                act.dma_start(row[0:BP, 0:width],
                              vec[name].rearrange("(a n) -> a n", a=1).to_broadcast([BP, width])
                              ).then_inc(params_loaded, 16)

            def attention(q, first, later):
                for args in first:
                    load_row(*args)
                n = [0]

                def read_product(residual, piece, m):
                    g = q.gemm0 + n[0]
                    act.wait_ge(gemm_done, g + 1)
                    b = bank(gemm_bank(q, g), 0, q.pieces[piece][1])
                    if residual:
                        a, width = q.pieces[piece]
                        ins = nc.scalar.activation(mem.resid[0:BP, m, a:a + width], b, ACT.Copy)
                    else:
                        a, width = q.pieces[piece]
                        if a % q.c == 0 and width % q.c == 0:
                            ins = nc.scalar.activation(feat(q, m, a // q.c, (a + width) // q.c),
                                                       b.rearrange("p (h c) -> p h c", c=q.c), ACT.Copy)
                        else:
                            for h, p, e, off in features_of(q, (a, width)):
                                ins = nc.scalar.activation(feat_flat(q, m, h * q.w + p, h * q.w + e),
                                                           b[:, off:off + e - p], ACT.Copy)
                    ins.then_inc(gemm_read, 1)
                    n[0] += 1

                for piece in range(len(q.pieces)):
                    for m in range(NB):
                        read_product(False, piece, m)
                if q.residual:
                    for piece in range(len(q.pieces)):
                        for m in range(NB):
                            read_product(True, piece, m)
                act.wait_ge(al_ready, (q.head0 + q.heads) * 2 * NB)
                for args in later:
                    load_row(*args)

                def read_rows(h):
                    act.wait_ge(rows_done, q.head0 + h + 1)
                    if h >= 2:
                        act.wait_ge(arg_ready, (q.head0 + h - 1) * NB)
                    nc.scalar.activation(mem.rows[0:BP, h % 2, :], ps[0:BP, 2560:2560 + 2 * N], ACT.Copy
                                         ).then_inc(rows_read, 1)

                read_rows(0)
                for h in range(q.heads):
                    if h + 1 < q.heads:
                        read_rows(h + 1)
                    for k in range(NB):
                        j = (q.head0 + h) * NB + k
                        act.wait_ge(arg_ready, j + 1)
                        t = mem.score[0:BP, (h * NB + k) % 3, :]
                        nc.scalar.activation(t, t, ACT.Exp).then_inc(exp_done, 1)

            par = mem.par
            turn_hi(T_Q[0], KC, mem.xh, ACT.Copy)
            act.wait_ge(gcn_ready, 4)
            attention(Q0, [("L2_gnn_a_src1", par[0], HID), ("L2_gnn_a_dst1", par[1], HID),
                           ("L2_gnn_be1", par[2], HID), ("L2_gnn_br1", par[3], HID)],
                      [("L2_gnn_b1", par[0], HID), ("L2_gnn_g1", par[1], HID)])
            layer_std(2)
            turn_hi(T_Q[1], K8, mem.xh8, ACT.Copy)
            attention(Q1, [("L2_gnn_a_src2", par[0], D), ("L2_gnn_a_dst2", mem.par0b, D),
                           ("L2_gnn_b2", par[1], D), ("L2_gnn_br2", par[3], D)],
                      [("L2_gnn_g2", par[0], D), ("L2_gnn_be2", mem.par0b, D)])
            layer_std(3)
            layer_std(4)
            turn_hi(T_Q[2], KC, mem.xh, ACT.Copy)
            attention(Q2, [("L3_gnn_a_src1", par[0], D), ("L3_gnn_a_dst1", mem.par0b, D),
                           ("L3_gnn_b1", par[1], D)], [])
            for m in range(NB):
                act.wait_ge(elu_in, m + 1)
                t = mem.feat[0:BP, m * D:(m + 1) * D]
                nc.scalar.activation(t, t, ACT.Exp).then_inc(elu_out, 1)
            turn_hi(T_Q[3], KC, mem.xh, ACT.Copy)
            attention(Q3, [("L3_gnn_a_src2", par[0], D), ("L3_gnn_a_dst2", mem.par0b, D),
                           ("L3_gnn_b2", par[1], D)], [])
            layer_std(5)

        @block.vector
        def _(dve):
            steps = [0]

            def link(ins):
                steps[0] += 1
                ins.then_inc(vchain, 1)
                dve.wait_ge(vchain, steps[0])

            def turn_lo(u0, k, dst_hi, dst_lo, relu):
                for u, unit in enumerate(turn_units(k)):
                    dve.wait_ge(xT_hi_ready, u0 + u + 1)
                    o, i, h = unit_out(dst_lo, unit), unit_in(u % 8, unit), unit_out(dst_hi, unit).bitcast(F32)
                    if relu:
                        ins = nc.vector.scalar_tensor_tensor(o, i, 0.0, h, ALU.max, ALU.subtract)
                    else:
                        ins = nc.vector.tensor_tensor(o, i, h, ALU.subtract)
                    ins.then_inc(xT_lo_ready, 1)

            dve.wait_ge(edges_loaded, 48)
            for t in (mem.src_f, mem.dst_f, mem.typ_f):
                nc.vector.memset(t[:, :], -1.0)
            link(nc.vector.memset(mem.cnt[:, :, :, :].rearrange("p r m n -> p (r m n)"), 0.0))
            nc.vector.memset(mem.sweep[:, 1, :, :], 0).then_inc(decoded, 1)
            for i, t in enumerate((mem.src_f, mem.dst_f, mem.typ_f)):
                ins = nc.vector.tensor_copy(t[0:BP, 0:ET], mem.edges_i[0:BP, i, :])
            link(ins)
            link(nc.vector.tensor_scalar(mem.tmp_f[0:BP, :], mem.typ_f[0:BP, :], 1.0, None, ALU.is_equal))
            link(nc.vector.scalar_tensor_tensor(mem.val_f[0:BP, :], mem.typ_f[0:BP, :], 3.0, mem.tmp_f[0:BP, :],
                                                ALU.is_equal, ALU.add))
            link(nc.vector.tensor_scalar(mem.val_f[0:BP, :], mem.val_f[0:BP, :], PAIR_BASE - 1.0, 1.0, ALU.mult, ALU.add))
            link(nc.vector.tensor_scalar(mem.dst_f[0:BP, :], mem.dst_f[0:BP, :], 1.0, None, ALU.add))
            for p, op in enumerate((ALU.is_lt, ALU.is_ge)):
                link(nc.vector.scalar_tensor_tensor(mem.dstp_f[0:BP, p, :], mem.typ_f[0:BP, :], 2.0,
                                                    mem.dst_f[0:BP, :], op, ALU.mult))
                link(nc.vector.tensor_scalar(mem.dstp_f[0:BP, p, :], mem.dstp_f[0:BP, p, :], 1.0, None, ALU.subtract))
            dve.wait_ge(consts_ready, 2)
            turn_lo(0, KC, mem.xh, mem.xl, False)

            def decode(s, k, before):
                m, step = k // 4, k % 4
                odd = mem.odd[0:BP, m % 2, :]
                both = mem.sweep[0:BP, s, m, :]
                if step == 0:
                    ins = nc.vector.tensor_scalar(odd, both, 12, None, ALU.logical_shift_right)
                elif step == 1:
                    ins = nc.vector.tensor_scalar(both, both, PAIR_BASE - 1, None, ALU.bitwise_and)
                elif step == 2:
                    dve.wait_ge(decoded, before)
                    c = mem.cnt[0:BP, 2 * s + 1, m, :]
                    ins = nc.vector.tensor_tensor(c, c, odd, ALU.add)
                else:
                    dve.wait_ge(decoded, before)
                    c = mem.cnt[0:BP, 2 * s, m, :]
                    ins = nc.vector.tensor_tensor(c, c, both, ALU.add)
                return ins.then_inc(decoded, 1)

            with dve.Fori(0, CHUNKS) as c:
                for p in range(2):
                    for t in range(SWEEP):
                        n, slot = p * SWEEP + t, (p * SWEEP + t) % OH_RING
                        dve.wait_ge(onehot_used, c * (2 * SWEEP) + max(n - OH_RING + 2, 0) + 1)
                        col = bass.ds(c * SWEEP + t, 1)
                        nc.vector.tensor_scalar(mem.oh_src[0:BP, slot, :], mem.iota[0:BP, :], mem.src_f[0:BP, col],
                                                mem.val_f[0:BP, col], ALU.is_equal, ALU.mult)
                        nc.vector.tensor_scalar(mem.oh_dst[0:BP, slot, :], mem.iota[0:BP, :], mem.dstp_f[0:BP, p, col],
                                                None, ALU.is_equal).then_inc(onehot_ready, 1)
                        if 2 <= t < 22:
                            if t == 2:
                                dve.wait_ge(sweep_read, c * 14 + 7 * p + 1)
                            decode(1 - p, t - 2, c * 40 + (20 * p + t - 2))
            dve.wait_ge(sweep_read, CHUNKS * 14 + 1)
            for k in range(20):
                decode(1, k, CHUNKS * 40 + k)

            def row3(ap):
                return ap.unsqueeze(1).to_broadcast([BP, NB, N])

            dve.wait_ge(decoded, CHUNKS * 40 + 20 + 1)
            t0, t1 = mem.sweep[0:BP, 0, :, :].bitcast(F32), mem.sweep[0:BP, 1, :, :].bitcast(F32)
            nc.vector.tensor_tensor(t0, mem.cnt[0:BP, 0, :, :], mem.cnt[0:BP, 1, :, :], ALU.add)
            link(nc.vector.tensor_tensor(t1, mem.cnt[0:BP, 2, :, :], mem.cnt[0:BP, 3, :, :], ALU.add))
            link(nc.vector.tensor_tensor(mem.ctot[0:BP, :, :], t0, t1, ALU.add))
            for r in range(NREL):
                inv = mem.inv[0:BP, r, :]
                dve.wait_ge(degree_done, r + 1)
                link(nc.vector.tensor_scalar(inv, ps[0:BP, r * 1024:r * 1024 + N], 1.0, None, ALU.max))
                nc.vector.reciprocal(inv, inv).then_inc(inv_ready, 1)
                dve.wait_ge(inv_ready, r + 1)
                c = mem.cnt[0:BP, r, :, :]
                nc.vector.tensor_tensor(c, c, row3(inv), ALU.mult).then_inc(adj_scaled, 1)
            for r in range(NREL):
                dve.wait_ge(adj_hi_ready, r + 1)
                nc.vector.tensor_tensor(mem.al[0:BP, r, :, :], mem.cnt[0:BP, r, :, :],
                                        mem.ah[0:BP, r, :, :].bitcast(F32), ALU.subtract).then_inc(adj_lo_ready, 1)

            def h_lo(i, slot, scale=None):
                dve.wait_ge(h_hi_ready, i + 1)
                o, p, h = mem.hl[0:BP, slot, :], bank(5 + slot, 0, HW), mem.hh[0:BP, slot, :].bitcast(F32)
                if scale is None:
                    nc.vector.tensor_tensor(o, p, h, ALU.subtract).then_inc(h_lo_ready, 1)
                else:
                    nc.vector.scalar_tensor_tensor(o, p, scale, h, ALU.mult, ALU.subtract).then_inc(h_lo_ready, 1)

            dve.wait_ge(bias_loaded, 16)
            with dve.Fori(0, RLAYERS) as l:
                for f in range(2):
                    for i in range(H_LAYER // 2):
                        n = f * (H_LAYER // 2) + i
                        h_lo(l * H_LAYER + n, n % 2)
                    for m in range(NB):
                        dve.wait_ge(out_done, l * 10 + (f * NB + m + 1))
                        nc.vector.tensor_tensor(mem.xn[0:BP, m:m + 1, f * HW:(f + 1) * HW],
                                                bank(m, 0, HW).unsqueeze(1),
                                                mem.bias0[0:BP, bass.ds(l, 1), f * HW:(f + 1) * HW],
                                                ALU.add).then_inc(out_read, 1)
                turn_lo(l * UNITS + UNITS, KC, mem.xh, mem.xl, True)

            def stats(m, t):
                for f in range(2):
                    ins = nc.vector.bn_stats(mem.stats[0:BP, m, f, :], t[0:BP, m, f * HW:(f + 1) * HW])
                link(ins)
                return nc.vector.bn_aggr(mem.mv[0:BP, m, :], mem.stats[0:BP, m, :, :])

            def add_and_norm(n):
                for m in range(NB):
                    link(nc.vector.tensor_tensor(mem.xn[0:BP, m, :], mem.xn[0:BP, m, :], mem.xres[0:BP, m, :], ALU.add))
                    ins = stats(m, mem.xn)
                link(ins)
                nc.vector.tensor_scalar(mem.std[0:BP, :], mem.mv[0:BP, :, 1], LN_EPS, None, ALU.add).then_inc(var_ready, 1)
                dve.wait_ge(std_ready, n + 1)
                link(nc.vector.reciprocal(mem.std[0:BP, :], mem.std[0:BP, :]))
                for m in range(NB):
                    nc.vector.tensor_scalar(mem.xres[0:BP, m, :], mem.xn[0:BP, m, :], mem.mv[0:BP, m, 0:1],
                                            mem.std[0:BP, m:m + 1], ALU.subtract, ALU.mult).then_inc(normed, 1)

            dve.wait_ge(out_read, 10 * RLAYERS)
            dve.wait_ge(res_loaded, 16)
            add_and_norm(0)
            turn_lo(T_L1, KC, mem.xh, mem.xl, False)
            link(nc.vector.tensor_copy(mem.cf[0:BP, :, :], mem.ctot[0:BP, :, :]))
            for m in range(NB):
                v = mem.cf[0:BP, m, nodes(m)]
                ins = nc.vector.tensor_tensor(v, v, mem.ident[0:BP, 0:BP], ALU.add)
            ins.then_inc(gcn_ready, 1)
            dve.wait_ge(gdeg_done, 1)
            nc.vector.tensor_copy(mem.deg[0:BP, :], bank(7, 0, NB)).then_inc(gdeg_ready, 1)
            dve.wait_ge(gsqrt_ready, 1)
            nc.vector.reciprocal(mem.dinv[0:BP, :], mem.deg[0:BP, :]).then_inc(dinv_ready, 1)
            dve.wait_ge(gcn_ready, 2)
            nc.vector.tensor_tensor(mem.cl[0:BP, :, :], mem.cf[0:BP, :, :], mem.ch[0:BP, :, :].bitcast(F32),
                                    ALU.subtract).then_inc(gcn_ready, 1)
            dve.wait_ge(dinv_ready, 1)
            dve.wait_ge(bias_loaded, 32)

            def masks(m):
                dve.wait_ge(mask_done, m + 1)
                if m:
                    dve.wait_ge(mask_read, m)
                row = ps[0:BP, (m % 2) * 1024:(m % 2) * 1024 + N]
                nc.vector.tensor_scalar(mem.mask_loop[0:BP, m, :], row, 0.0, NEG, ALU.is_equal, ALU.mult)
                link(nc.vector.tensor_tensor(mem.diag[0:BP, :], row[:, nodes(m)], mem.ident[0:BP, 0:BP],
                                             ALU.subtract))
                link(nc.vector.tensor_scalar(mem.mask_plain[0:BP, m, :], row, 0.0, NEG, ALU.is_equal, ALU.mult))
                nc.vector.tensor_scalar(mem.mask_plain[0:BP, m, nodes(m)], mem.diag[0:BP, :], 0.0, NEG,
                                        ALU.is_equal, ALU.mult).then_inc(mask_read, 1)

            masks(0)
            masks(1)
            for layer in range(2):
                for f in range(2):
                    for i in range(NB):
                        if layer == 0 and f == 0 and i == 1:
                            for m in range(2, NB):
                                masks(m)
                        h_lo(H_L1 + layer * 2 * NB + f * NB + i, (f * NB + i) % 2, mem.dinv[0:BP, i:i + 1])
                    for m in range(NB):
                        dve.wait_ge(out_done, RLAYERS * 10 + (layer * 2 + f) * NB + m + 1)
                        nc.vector.scalar_tensor_tensor(mem.xn[0:BP, m, f * HW:(f + 1) * HW], bank(m, 0, HW),
                                                       mem.dinv[0:BP, m:m + 1],
                                                       mem.bias1[0:BP, layer, f * HW:(f + 1) * HW],
                                                       ALU.mult, ALU.add).then_inc(out_read, 1)
                if layer == 0:
                    turn_lo(T_L1 + UNITS, KC, mem.xh, mem.xl, True)
            dve.wait_ge(out_read, RLAYERS * 10 + 20)
            add_and_norm(1)

            def attention(q, bias_row, src_row, dst_row, dest, first, all_rows):
                P0 = q.head0 * NB
                mask = mem.mask_loop if q.loops else mem.mask_plain
                cnt = mem.cnt_loop if q.loops else mem.ctot
                v = mem.feat[0:BP, 0:NB * q.heads * q.w].rearrange("p (h w) -> p h w", w=q.w)
                link(nc.vector.memset(v[:, :, q.c:q.w], 1.0))
                dve.wait_ge(params_loaded, 16 * first)
                scratch = mem.score[0:BP, :, :].rearrange("p a n -> p (a n)")
                for h in range(q.heads):
                    last_piece = next(i for i, (a, w) in enumerate(q.pieces) if (h + 1) * q.c <= a + w)
                    for m in range(NB):
                        dve.wait_ge(gemm_read, q.gemm0 + last_piece * NB + m + 1)
                        for j, row, o in ((0, src_row, mem.al_src), (1, dst_row, mem.al_dst)):
                            done = 2 * ((q.head0 + h) * NB + m) + j
                            if 2 * (h * NB + m) + j >= 2:
                                dve.wait_ge(al_ready, done - 1)
                            nc.vector.tensor_tensor_reduce(
                                out=scratch[:, done % 2 * D:done % 2 * D + q.c], in0=feat_flat(q, m, h * q.w, h * q.w + q.c),
                                in1=row[0:BP, h * q.c:(h + 1) * q.c], scale=1.0, scalar=0.0, op0=ALU.mult,
                                op1=ALU.add, accum_out=o[0:BP, m, h:h + 1]).then_inc(al_ready, 1)
                dve.wait_ge(al_ready, (q.head0 + q.heads) * 2 * NB)
                for h in range(q.heads):
                    dve.wait_ge(max_row_done, q.head0 + h + 1)
                    row = ps[0:BP, (h % 2) * 1024:(h % 2) * 1024 + N]
                    for m in range(NB):
                        done = (q.head0 + h) * NB + m
                        if h * NB + m >= 3:
                            dve.wait_ge(max_done, done - 2)
                        nc.vector.tensor_tensor_reduce(
                            out=mem.score[0:BP, done % 3, :], in0=row, in1=mask[0:BP, m, :], scale=1.0, scalar=-3.0e38,
                            op0=ALU.add, op1=ALU.max, accum_out=mem.al_max[0:BP, m, h:h + 1]
                        ).then_inc(max_done, 1)
                dve.wait_ge(max_done, (q.head0 + q.heads) * NB)

                def cols(t):
                    return t[0:BP, :, 0:q.heads]

                u, m_ = cols(mem.al_sum), cols(mem.al_max)
                link(nc.vector.tensor_tensor(u, m_, cols(mem.al_dst), ALU.add))
                link(nc.vector.scalar_tensor_tensor(m_, u, SLOPE, u, ALU.mult, ALU.max))
                nc.vector.tensor_tensor(cols(mem.row1), cols(mem.al_dst), m_, ALU.subtract)
                nc.vector.tensor_scalar(cols(mem.al_src2), cols(mem.al_src), SLOPE, None, ALU.mult)
                nc.vector.scalar_tensor_tensor(cols(mem.row2), cols(mem.al_dst), SLOPE, m_, ALU.mult, ALU.subtract
                                               ).then_inc(cols_ready, 1)

                def probs(j):
                    dve.wait_ge(exp_done, P0 + j + 1)
                    if j >= q.ring:
                        h, k = (j - q.ring) // NB, (j - q.ring) % NB
                        if k == NB - 1:
                            dve.wait_ge(part_done, (q.part0 + h + 1) * NB)
                        else:
                            dve.wait_ge(prob_used, (q.head0 + h) * (NB - 1) + k + 1)
                    nc.vector.scalar_tensor_tensor(mem.prob[0:BP, j % q.ring, :], mem.score[0:BP, j % 3, :], 1.0,
                                                   cnt[0:BP, j % NB, :], ALU.min, ALU.mult).then_inc(prob_ready, 1)

                def read_part(i):
                    h, a, width = q.parts[i]
                    dve.wait_ge(part_done, (q.part0 + i + 1) * NB)
                    if a + width == (h + 1) * q.w:
                        z = ps[0:BP, 0:NB * 512].rearrange("p (m n) -> p m n", m=NB)[:, :, width - 1]
                        link(nc.vector.tensor_scalar(mem.z[0:BP, :], z, 1e-16, None, ALU.add))
                        link(nc.vector.reciprocal(mem.z[0:BP, :], mem.z[0:BP, :]))
                        width -= 1
                    for m in range(NB):
                        b0 = a - h * (q.w - q.c)
                        nc.vector.scalar_tensor_tensor(dest(m, h, a, width), bank(m, 0, width), mem.z[0:BP, m:m + 1],
                                                       bias_row[0:BP, b0:b0 + width], ALU.mult, ALU.add
                                                       ).then_inc(part_read, 1)

                dve.wait_ge(params_loaded, 16 * all_rows)
                n = q.heads * NB
                for j in range(n + 2):
                    h, k = j // NB, j % NB
                    if k == 3 and h >= 1:
                        read_part(h - 1)
                    if j < n:
                        slot = j % 3
                        if k == 0:
                            dve.wait_ge(rows_read, q.head0 + h + 1)
                        t = mem.score[0:BP, slot, :]
                        if j >= 3:
                            dve.wait_ge(prob_ready, P0 + j - 2)
                        steps[0] += 1
                        flat = steps[0]
                        nc.vector.tensor_scalar(t, mem.rows[0:BP, h % 2, N:2 * N], mem.al_src2[0:BP, k, h:h + 1],
                                                None, ALU.add).then_inc(vchain, 1)
                    if j >= 2:
                        probs(j - 2)
                    if j < n:
                        dve.wait_ge(vchain, flat)
                        nc.vector.scalar_tensor_tensor(t, mem.rows[0:BP, h % 2, 0:N], mem.al_src[0:BP, k, h:h + 1],
                                                       t, ALU.add, ALU.max).then_inc(arg_ready, 1)
                for i in range(q.heads - 1, len(q.parts)):
                    read_part(i)
                dve.wait_ge(part_read, (q.part0 + len(q.parts)) * NB)

            def norm_rows(n, block, halves, width):
                for m in range(NB):
                    for f in range(2):
                        ins = nc.vector.bn_stats(mem.stats[0:BP, m, f, :], halves(m, f))
                    link(ins)
                    ins = nc.vector.bn_aggr(mem.mv[0:BP, m, :], mem.stats[0:BP, m, :, :])
                link(ins)
                nc.vector.tensor_scalar(mem.std[0:BP, :], mem.mv[0:BP, :, 1], LN_EPS, None, ALU.add).then_inc(var_ready, 1)
                dve.wait_ge(std_ready, n + 1)
                link(nc.vector.reciprocal(mem.std[0:BP, :], mem.std[0:BP, :]))
                for m in range(NB):
                    t = block(m)
                    link(nc.vector.tensor_scalar(t, t, mem.mv[0:BP, m, 0:1], mem.std[0:BP, m:m + 1],
                                                 ALU.subtract, ALU.mult))

            nc.vector.tensor_copy(mem.cnt_loop[0:BP, :, :], mem.cf[0:BP, :, :]).then_inc(gcn_ready, 1)
            turn_lo(T_Q[0], KC, mem.xh, mem.xl, False)

            def in_place(q):
                return lambda m, h, a, width: feat_flat(q, m, a, a + width)

            attention(Q0, mem.par[0], mem.par[0], mem.par[1], in_place(Q0), 4, 6)
            norm_rows(2, lambda m: feat(Q0, m), lambda m, f: feat(Q0, m, 2 * f, 2 * f + 2), HID)

            def by_heads(row):
                return row[0:BP, 0:HID].rearrange("p (h c) -> p h c", h=HEADS2)

            for m in range(NB):
                t = feat(Q0, m)
                link(nc.vector.tensor_tensor(t, t, by_heads(mem.par[1]), ALU.mult))
                link(nc.vector.tensor_tensor(t, t, by_heads(mem.par[2]), ALU.add))
                dve.wait_ge(bias_added, m + 1)
                nc.vector.scalar_tensor_tensor(t, t, 0.0, by_heads(mem.resid[:, m, :]), ALU.max, ALU.add
                                               ).then_inc(layer_ready, 1)
            turn_lo(T_Q[1], K8, mem.xh8, mem.xl8, False)
            attention(Q1, mem.par[1], mem.par[0], mem.par0b, in_place(Q1), 10, 12)
            norm_rows(3, lambda m: feat_flat(Q1, m, 0, D), lambda m, f: feat_flat(Q1, m, f * HW, (f + 1) * HW), D)
            for m in range(NB):
                t = feat_flat(Q1, m, 0, D)
                link(nc.vector.tensor_tensor(t, t, mem.par[0][0:BP, 0:D], ALU.mult))
                link(nc.vector.tensor_tensor(t, t, mem.par0b[0:BP, :], ALU.add))
                dve.wait_ge(bias_added, NB + 2 * (m + 1))
                link(nc.vector.tensor_tensor(t, t, mem.resid[0:BP, m, 0:D], ALU.add))
            norm_rows(4, lambda m: feat_flat(Q1, m, 0, D), lambda m, f: feat_flat(Q1, m, f * HW, (f + 1) * HW), D)
            for m in range(NB):
                nc.vector.tensor_copy(mem.xres[0:BP, m, :], feat_flat(Q1, m, 0, D)).then_inc(normed, 1)
            turn_lo(T_Q[2], KC, mem.xh, mem.xl, False)
            hn = mem.resid[0:BP, :, 0:D]
            attention(Q2, mem.par[1], mem.par[0], mem.par0b,
                      lambda m, h, a, width: hn[:, m, h * C3:(h + 1) * C3], 15, 15)
            for m in range(NB):
                nc.vector.tensor_scalar(mem.feat[0:BP, m * D:(m + 1) * D], hn[:, m, :], 0.0, None, ALU.min
                                        ).then_inc(elu_in, 1)
            for m in range(NB):
                link(nc.vector.tensor_scalar(hn[:, m, :], hn[:, m, :], 0.0, None, ALU.max))
                dve.wait_ge(elu_out, m + 1)
                nc.vector.scalar_tensor_tensor(hn[:, m, :], mem.feat[0:BP, m * D:(m + 1) * D], 1.0, hn[:, m, :],
                                               ALU.subtract, ALU.add).then_inc(layer_ready, 1)
            turn_lo(T_Q[3], KC, mem.xh, mem.xl, False)
            attention(Q3, mem.par[1], mem.par[0], mem.par0b,
                      lambda m, h, a, width: mem.xn[0:BP, m, a:a + width], 18, 18)
            add_and_norm(5)

        @block.tensor
        def _(pe):

            def of(t):
                return lambda m, c: t[0:BP, m, c * 128:(c + 1) * 128]

            def turn(k, column, u0=0):
                for u, unit in enumerate(turn_units(k)):
                    if u >= 8:
                        pe.wait_ge(xT_lo_ready, u0 + u - 7)
                    for j, (c, m) in enumerate(unit):
                        ins = nc.tensor.transpose(ps[:, (u % 8) * 512 + j * BP:(u % 8) * 512 + (j + 1) * BP],
                                                  column(m, c), mem.ident[0:BP, 0:BP])
                    ins.then_inc(turned, 1)

            def gemm_block(o, xh, xl, m, k, c, static, width, stop, owed=False):
                for j in range(k):
                    if m == 0:
                        pe.wait_ge(w_lo_ready, c + (j + 1))
                    slot = (static + j) % WRING
                    h, l, wh, wl = xh[:, j, nodes(m)], xl[:, j, nodes(m)], mem.wh[:, slot, 0:width], mem.wl[:, slot, 0:width]
                    ins = nc.tensor.matmul(o, h, wl, start=(j == 0), stop=False, skip_group_check=True)
                    if owed and j == 0:
                        ins.then_inc(w_used, 1)
                    nc.tensor.matmul(o, l, wh, start=False, stop=False, skip_group_check=True)
                    ins = nc.tensor.matmul(o, h, wh, start=False, stop=stop and j == k - 1, skip_group_check=True)
                    if m == NB - 1 and j < k - 1:
                        ins.then_inc(w_used, 1)
                return ins

            def aggregate(adj_h, adj_l, s, slot, i, start, stop, after_gemm, free=None):
                pe.wait_ge(h_lo_ready, i + 1)
                for m in range(NB):
                    if free is not None:
                        pe.wait_ge(out_read, free + m + 1)
                    o, ah, al = bank(m, 0, HW), adj_h[0:BP, s, nodes(m)], adj_l[0:BP, s, nodes(m)]
                    ins = nc.tensor.matmul(o, ah, mem.hl[0:BP, slot, :], start=start, stop=False, skip_group_check=True)
                    if after_gemm and m == 0:
                        ins.then_inc(w_used, 1)
                    nc.tensor.matmul(o, al, mem.hh[0:BP, slot, :], start=False, stop=False, skip_group_check=True)
                    ins = nc.tensor.matmul(o, ah, mem.hh[0:BP, slot, :], start=False, stop=stop, skip_group_check=True)
                    if stop:
                        ins.then_inc(out_done, 1)
                if not stop:
                    ins.then_inc(agg_used, 1)

            def agg1(layer, f, s, after_gemm):
                n = f * NB + s
                if layer == 0 and n == 0:
                    pe.wait_ge(gcn_ready, 3)
                    pe.wait_ge(mask_read, NB)
                aggregate(mem.ch, mem.cl, s, n % 2, H_L1 + layer * 2 * NB + n, s == 0, s == NB - 1, after_gemm,
                          RLAYERS * 10 + layer * 10 if s == 0 and f else None)

            pe.wait_ge(consts_ready, 2)
            pe.wait_ge(x_loaded, 16)
            turn(KC, of(mem.xn))
            pe.wait_ge(xT_lo_ready, UNITS)

            pe.sem_inc(onehot_used, 1)
            with pe.Fori(0, CHUNKS) as c:
                for p in range(2):
                    for t in range(SWEEP):
                        slot = (p * SWEEP + t) % OH_RING
                        pe.wait_ge(onehot_ready, c * (2 * SWEEP) + (p * SWEEP + t + 1))
                        first, last = t == 0, t == SWEEP - 1
                        for j, (b, a, e) in enumerate(SWEEP_BANKS):
                            if first:
                                pe.wait_ge(sweep_read, c * 14 + p * (j + 1) + 1)
                            ms = range(4) if b == 5 else [4] if b == 6 else [b]
                            for m in ms:
                                o = bank(b, m % 4 * TAIL, m % 4 * TAIL + TAIL) if b >= 5 else bank(b)
                                ins = nc.tensor.matmul(o, mem.oh_src[0:BP, slot, nodes(m)], mem.oh_dst[0:BP, slot, a:e],
                                                       start=first and (b != 5 or m == 0), stop=last,
                                                       skip_group_check=True)
                                if b == 5 and m == 0:
                                    ins.then_inc(onehot_used, 1)
                            if last:
                                ins.then_inc(sweep_done, 1)

            pe.wait_ge(sweep_read, 14 * CHUNKS + 1)
            ones = mem.ones[0:BP, 0:1].to_broadcast([BP, BP])
            for m in range(NB):
                pe.wait_ge(decoded, CHUNKS * 40 + 4 * (m + 1) + 1)
                for r in range(NREL):
                    for a, e in ((0, 512), (512, N)):
                        ins = nc.tensor.matmul(ps[0:BP, r * 1024 + a:r * 1024 + e], ones, mem.cnt[0:BP, r, m, a:e],
                                               start=(m == 0), stop=(m == NB - 1))
                    if m == NB - 1:
                        ins.then_inc(degree_done, 1)
            pe.wait_ge(inv_ready, NREL)

            with pe.Fori(0, RLAYERS) as l:
                pe.wait_ge(xT_lo_ready, l * UNITS + UNITS)
                for f in range(2):
                    static = f * (L0_CHUNKS // 2)
                    c = l * L0_CHUNKS + static
                    for m in range(NB):
                        if f == 1:
                            pe.wait_ge(out_read, l * 10 + (m + 1))
                        ins = gemm_block(bank(m, 0, HW), mem.xh, mem.xl, m, KC, c, static, HW, False)
                    ins.then_inc(w_used, 1)

                    def agg(i, after_gemm):
                        r, s = i // NB, i % NB
                        if s == 0:
                            pe.wait_ge(adj_lo_ready, r + 1)
                        n = f * (H_LAYER // 2) + i
                        aggregate(mem.ah[:, r], mem.al[:, r], s, n % 2, l * H_LAYER + n, False,
                                  i == H_LAYER // 2 - 1, after_gemm)

                    for i in range(H_LAYER // 2):
                        r, s = i // NB, i % NB
                        n = f * (H_LAYER // 2) + i
                        if n >= 2:
                            pe.wait_ge(h_lo_ready, l * H_LAYER + (n - 1))
                        k0 = KC * (1 + r)
                        gemm_block(bank(5 + n % 2, 0, HW), mem.xh, mem.xl, s, KC, c + k0, static + k0, HW, True
                                   ).then_inc(h_done, 1)
                        if i:
                            agg(i - 1, s == NB - 1)
                    agg(H_LAYER // 2 - 1, False)
                pe.wait_ge(out_read, l * 10 + 10)
                turn(KC, of(mem.xn))

            pe.wait_ge(normed, NB)
            turn(KC, of(mem.xres))
            pe.wait_ge(gcn_ready, 1)
            pe.wait_ge(xT_lo_ready, T_L1 + UNITS)
            for m in range(NB):
                for s in range(NB):
                    ins = nc.tensor.matmul(bank(7, m, m + 1), mem.cf[0:BP, s, nodes(m)], mem.ones[0:BP, 0:1],
                                           start=(s == 0), stop=(s == NB - 1))
            ins.then_inc(gdeg_done, 1)
            def mask_row(m):
                if m >= 2:
                    pe.wait_ge(mask_read, m - 1)
                off = (m % 2) * 1024
                for s, p, e, a, z in score_pieces(off):
                    ins = nc.tensor.matmul(ps[0:BP, p:e], mem.cf[0:BP, s, nodes(m)], mem.ident[0:BP, a:z],
                                           start=True, stop=True)
                ins.then_inc(mask_done, 1)

            mask_row(0)
            mask_row(1)
            for layer in range(2):
                if layer:
                    pe.wait_ge(out_read, RLAYERS * 10 + 10)
                    turn(KC, of(mem.xn))
                    pe.wait_ge(xT_lo_ready, T_L1 + 2 * UNITS)
                for f in range(2):
                    c = BASE_L1 + (layer * 2 + f) * KC
                    for s in range(NB):
                        n = f * NB + s
                        if n >= 2:
                            pe.wait_ge(h_lo_ready, H_L1 + layer * 2 * NB + n - 1)
                        if layer == 0 and n == 1:
                            for m in range(2, NB):
                                mask_row(m)
                        gemm_block(bank(5 + n % 2, 0, HW), mem.xh, mem.xl, s, KC, c, c, HW, True).then_inc(h_done, 1)
                        if s:
                            agg1(layer, f, s - 1, s == NB - 1)
                    agg1(layer, f, NB - 1, False)

            def attention(q, xh, xl, u):
                pe.wait_ge(xT_lo_ready, u)
                mark = [0, False]

                def product_of(piece, m, residual):
                    g = q.gemm0 + mark[0]
                    if mark[0] >= 3:
                        pe.wait_ge(gemm_read, g - 2)
                    a, width = q.pieces[piece]
                    c = q.chunk + ((len(q.pieces) if residual else 0) + piece) * q.k
                    gemm_block(bank(gemm_bank(q, g), 0, width), xh, xl, m, q.k, c, c, width, True, mark[1]
                               ).then_inc(gemm_done, 1)
                    mark[0] += 1
                    mark[1] = m == NB - 1

                def broadcast_row(t, h, off):
                    for m, p, e, a, z in score_pieces(off):
                        ins = nc.tensor.matmul(ps[0:BP, p:e], t[0:BP, m, h:h + 1].to_broadcast([BP, BP]),
                                               mem.ident[0:BP, a:z], start=True, stop=True)
                        if mark[1] and m == 0:
                            ins.then_inc(w_used, 1)
                            mark[1] = False
                    return ins

                for piece in range(len(q.pieces)):
                    for m in range(NB):
                        product_of(piece, m, False)
                todo = [(piece, m) for piece in range(len(q.pieces)) for m in range(NB)] if q.residual else []
                for h in range(q.heads + 1):
                    for _ in range(q.fill[h]):
                        product_of(*todo.pop(0), True)
                    if h < q.heads:
                        pe.wait_ge(al_ready, (q.head0 + h + 1) * 2 * NB)
                        if h >= 2:
                            pe.wait_ge(max_done, (q.head0 + h - 1) * NB)
                        broadcast_row(mem.al_src, h, (h % 2) * 1024).then_inc(max_row_done, 1)
                pe.wait_ge(cols_ready, q.index + 1)
                pe.wait_ge(gemm_read, q.gemm0 + mark[0])

                def rows_of(h):
                    if h:
                        pe.wait_ge(rows_read, q.head0 + h)
                    broadcast_row(mem.row1, h, 5 * 512)
                    broadcast_row(mem.row2, h, 5 * 512 + N).then_inc(rows_done, 1)

                def sum_block(i, k, used):
                    h, a, width = q.parts[i]
                    j = h * NB + k
                    for m in range(NB):
                        if k == 0 and i:
                            pe.wait_ge(part_read, (q.part0 + i - 1) * NB + m + 1)
                        ins = nc.tensor.matmul(bank(m, 0, width), mem.prob[0:BP, j % q.ring, nodes(m)],
                                               feat_flat(q, k, a, a + width), start=(k == 0), stop=(k == NB - 1))
                        if k == NB - 1:
                            ins.then_inc(part_done, 1)
                    if k < NB - 1 and used:
                        ins.then_inc(prob_used, 1)

                rows_of(0)
                for h in range(q.heads):
                    if h + 1 < q.heads:
                        rows_of(h + 1)
                    for k in range(NB):
                        pe.wait_ge(prob_ready, (q.head0 + h) * NB + k + 1)
                        sum_block(h, k, True)
                if q.heads == 1:
                    for k in range(NB):
                        sum_block(1, k, False)

            pe.wait_ge(normed, 2 * NB)
            turn(KC, of(mem.xres))
            attention(Q0, mem.xh, mem.xl, T_Q[1])
            pe.wait_ge(layer_ready, NB)
            turn(K8, lambda m, c: feat_flat(Q0, m, c // 2 * Q0.w + c % 2 * 128, c // 2 * Q0.w + c % 2 * 128 + 128),
                 T_Q[1])
            attention(Q1, mem.xh8, mem.xl8, T_Q[2])
            pe.wait_ge(normed, 3 * NB)
            turn(KC, of(mem.xres))
            attention(Q2, mem.xh, mem.xl, T_Q[3])
            pe.wait_ge(layer_ready, 2 * NB)
            turn(KC, of(mem.resid))
            attention(Q3, mem.xh, mem.xl, T_Q[3] + UNITS)


def lay_chunks(mats):
    import numpy as np
    out = []
    for w, pieces in mats:
        for a, width in pieces:
            for k in range(w.shape[0] // 128):
                c = np.zeros((128, HW), w.dtype)
                c[:, :width] = w[k * 128:(k + 1) * 128, a:a + width]
                out.append(c)
    return out


def weight_stream(i):
    import numpy as np
    chunks = []
    for layer in "123":
        w, root = i["L0_gnn_W" + layer], i["L0_gnn_root" + layer]
        for piece in PIECES:
            for m in [root] + [w[r] for r in range(NREL)]:
                chunks += lay_chunks([(m, [piece])])
    for n in ("L1_gnn_W1", "L1_gnn_W2"):
        chunks += lay_chunks([(i[n], PIECES)])
    for n in ("L2_gnn_W1", "L2_gnn_Wr1"):
        chunks += lay_chunks([(i[n], PIECES1)])
    for n in ("L2_gnn_W2", "L2_gnn_Wr2"):
        chunks += lay_chunks([(i[n], PIECES)])
    for n in ("L3_gnn_W1", "L3_gnn_W2"):
        chunks += lay_chunks([(i[n], PIECES)])
    return np.ascontiguousarray(np.stack(chunks))


VECTORS = ["L2_gnn_a_src1", "L2_gnn_a_dst1", "L2_gnn_b1", "L2_gnn_g1", "L2_gnn_be1", "L2_gnn_br1",
           "L2_gnn_a_src2", "L2_gnn_a_dst2", "L2_gnn_b2", "L2_gnn_g2", "L2_gnn_be2", "L2_gnn_br2",
           "L3_gnn_a_src1", "L3_gnn_a_dst1", "L3_gnn_b1", "L3_gnn_a_src2", "L3_gnn_a_dst2", "L3_gnn_b2"]


def kernel(**inputs):
    import numpy as np
    import concourse.bacc as bacc
    from concourse.bass_utils import run_bass_kernel_spmd as run
    i = {name: np.asarray(a) for name, a in inputs.items()}
    arrays = {
        "x_dram": i["x"], "src_dram": i["src"], "dst_dram": i["dst"], "edge_type_dram": i["edge_type_4"],
        "weights_dram": weight_stream(i),
        "rgcn_bias_dram": np.stack([i["L0_gnn_b" + layer] for layer in "123"]),
        "gcn_bias_dram": np.stack([i["L1_gnn_b1"], i["L1_gnn_b2"]]),
    }
    for name in VECTORS:
        arrays[name + "_dram"] = i[name].reshape(-1)
    arrays = {name: np.ascontiguousarray(a) for name, a in arrays.items()}
    nc = bacc.Bacc("TRN2", target_bir_lowering=False, num_devices=1)
    aps = [nc.dram_tensor(name, a.shape, mybir.dt.from_np(a.dtype), kind="ExternalInput").ap()
           for name, a in arrays.items()]
    out = nc.dram_tensor("out_dram", (N, D), F32, kind="ExternalOutput").ap()
    program(nc, *aps[:7], dict(zip(VECTORS, aps[7:])), out)
    r = run(nc, [arrays], core_ids=[0])
    return r.results[0]["out_dram"]
```

```python
from contextlib import ExitStack

import concourse.bass as bass
from concourse import mybir

F32 = mybir.dt.float32
F32R = mybir.dt.float32r
BF16 = mybir.dt.bfloat16
FP16 = mybir.dt.float16
I32 = mybir.dt.int32
I16 = mybir.dt.int16
ALU = mybir.AluOpType
ACT = mybir.ActivationFunctionType

N = 625
D = 768
E = 10000
BP = 125
NB = N // BP
KC = D // 128
HW = 384
NREL = 4
RLAYERS = 3
PAIR_BASE = 4096
ET = E // BP
SWEEP = 27
CHUNKS = -(-ET // SWEEP)
ETP = SWEEP * CHUNKS
HID = 1024
HEADS2, C2 = 4, 256
HEADS3, C3 = 8, 96
WRING = 10
LAST_TILES = 3
OH_RING = 6
RAW = 5
NEG = -1.0e30
LN_EPS = 1e-5
SLOPE = 0.2

L0_CHUNKS = 2 * KC * (NREL + 1)
PIECES1 = [(0, 384), (384, 384), (768, 256)]
PIECES = [(0, 384), (384, 384)]
K8 = HID // 128


def gemm_chunks(k, pieces):
    return k * len(pieces)


BASE_L1 = RLAYERS * L0_CHUNKS
BASE_L2 = BASE_L1 + 2 * gemm_chunks(KC, PIECES)
BASE_L2B = BASE_L2 + 2 * gemm_chunks(KC, PIECES1)
BASE_L3 = BASE_L2B + 2 * gemm_chunks(K8, PIECES)
NCHUNKS = BASE_L3 + 2 * gemm_chunks(KC, PIECES)
READ_ROWS = {(3, 0): 0, (4, 0): 1, (2, 1): 0}
ACT_SPLITS = (BASE_L2 + WRING - 1) // WRING * WRING
AHEAD = WRING - 1


class Attention:

    def __init__(self, before, heads, c, k, pieces, residual, chunk, loops):
        g = before
        self.index = g.index + 1 if g else 0
        self.heads, self.c, self.k, self.pieces, self.residual, self.chunk = heads, c, k, pieces, residual, chunk
        self.loops = loops
        self.w = c + 1
        if heads == 1:
            self.groups = [[(0, HW, HW + 1, 0)], [(0, 0, HW, 0)]]
        else:
            n = 512 // self.w
            n = max(i for i in range(1, n + 1) if heads % i == 0)
            self.groups = [[(h, h * self.w, self.w, (h - h0) * self.w) for h in range(h0, h0 + n)]
                           for h0 in range(0, heads, n)]
        self.per_group = len(self.groups[0])
        self.ring = 3 if self.index == 0 else 5
        self.gemm0 = g.gemm0 + len(g.banks) if g else 0
        self.al_parts = 2 if heads == 1 else 1
        self.al_head = 2 * NB * self.al_parts + (2 if self.al_parts == 2 else 0)
        self.al0 = g.al0 + g.heads * g.al_head if g else 0
        self.head0 = g.head0 + g.heads if g else 0
        self.group0 = g.group0 + len(g.groups) if g else 0
        self.used0 = g.used0 + (g.heads * NB - len(g.groups) if g.heads > 1 else 0) if g else 0
        n = len(pieces)
        self.banks = [b % 8 for b in range(NB * n)] + (list(range(NB)) * n if residual else [])
        self.end = chunk + (2 if residual else 1) * n * k
        self.max_at = {0: {15: 0, 22: 1}, 1: {11: 0}, 2: {3: 0}}.get(self.index, {})
        self.rows_at = {0: {19: 0, 26: 1}, 1: {17: 0}, 2: {5: 0}}.get(self.index, {})
        self.first = min(heads, 2)
        self.stored = self.index == 2
        self.half = heads // 2 if self.index == 2 else heads

    def rows_col(self, h):
        return 2 * 512 if self.index == 2 and h == 0 else 5 * 512

    def max_count(self, h):
        return (self.head0 + h + 1) - (HEADS3 - 2 if self.index == 3 else 0)

    def free_count(self, i):
        last = [j for j in range(i) if self.banks[j] == self.banks[i]]
        return self.gemm0 + last[-1] + 1 if last else 0

    def used_count(self, h, k):
        return self.used0 + h * NB + k + 1 - h // self.per_group


Q0 = Attention(None, HEADS2, C2, KC, PIECES1, True, BASE_L2, True)
Q1 = Attention(Q0, 1, D, K8, PIECES, True, BASE_L2B, True)
Q2 = Attention(Q1, HEADS3, C3, KC, PIECES, False, BASE_L3, False)
Q3 = Attention(Q2, 1, D, KC, PIECES, False, BASE_L3 + 2 * KC, False)


class Memory:

    def __init__(self, nc):
        base = (nc.sbuf_base + 63) // 64 * 64

        def at(name, shape, dt, offset):
            return nc.alloc_sbuf_tensor_at(name, shape, dt, offset=base + offset)

        self.ident = at("ident", [128, 128], F32, 0)
        self.ones = at("ones", [128, 16], F32, 512)
        small = 576
        wh = 2688
        wl = wh + WRING * HW * 4
        raw = wl + WRING * HW * 4
        x = raw + RAW * HW * 4
        xn = x + 30016
        ah = xn + D * NB * 4
        al = ah + 50016
        ci = al + 50016
        h = ci + 6272
        bias = h + 6144
        tail = bias + 9216
        assert base + tail + 4096 <= nc.sbuf_usable_end

        self.wh = at("w_hi", [128, WRING, HW], F32R, wh)
        self.wl = at("w_lo", [128, WRING, HW], F32R, wl)
        self.raw = at("w_raw", [128, RAW, HW], F32, raw)
        self.xh = at("xT_hi", [128, KC, N], F32R, x)
        self.xl = at("xT_lo", [128, KC, N], F32R, x + 15008)
        self.xn = at("x_nat", [128, NB, D], F32, xn)
        self.ah = at("adj_hi", [128, NREL, NB, N], F32R, ah)
        self.al = at("adj_lo", [128, NREL, NB, N], F32R, al)
        self.cnt = at("edge_counts", [128, NREL, NB, N], F32, al)
        self.ctot = at("counts_all", [128, NB, N], I16, ci)
        self.hh = at("h_hi", [128, 2, HW], F32R, h)
        self.hl = at("h_lo", [128, 2, HW], F32R, h + 2 * HW * 4)
        self.bias0 = at("rgcn_bias", [128, RLAYERS, D], F32, bias)

        self.sweep = at("sweep_sums", [128, 2, NB, N], I32, ah)
        self.odd = at("sweep_odd", [128, 2, N], I32, ah + 25024)
        self.oh_src = at("onehot_src", [128, OH_RING, N], BF16, ci)
        self.oh_dst = at("onehot_dst", [128, OH_RING, N], BF16, ah + 30080)
        self.iota = at("iota", [128, N], FP16, ah + 40192)
        edges = ah + 41472
        self.edges_i = at("edges_int", [128, 3, ET], I32, edges)
        self.src_f = at("src_f", [128, ETP], F32, edges + 960)
        self.dst_f = at("dst_f", [128, ETP], F32, edges + 1312)
        self.typ_f = at("typ_f", [128, ETP], F32, edges + 1664)
        self.val_f = at("val_f", [128, ETP], F32, edges + 2016)
        self.tmp_f = at("tmp_f", [128, ETP], F32, edges + 2368)
        self.dstp_f = at("dst_of_pair", [128, 2, ETP], F32, edges + 2720)
        self.inv = [at(f"inv_degree{r}", [128, N], F32, ah + 39520 + 2528 * r) for r in range(NREL - 1)]
        self.inv.append(at("inv_degree3", [128, N], F32, tail))

        self.stats = at("ln_stats", [128, NB, 2, 6], F32, small)
        self.mv = at("ln_mean_var", [128, NB, 2], F32, small + 256)
        self.std = at("ln_std", [128, NB], F32, small + 320)
        self.dinv = at("gcn_dinv", [128, NB], F32, small + 384)
        self.deg = at("gcn_deg", [128, NB], F32, small + 448)
        self.xres = at("x_residual", [128, NB, D], F32, ah)
        self.ch = at("gcn_counts_hi", [128, NB, N], F32R, ah + 15360)
        self.cl = at("gcn_counts_lo", [128, NB, N], F32R, ah + 27904)
        self.cf = at("gcn_counts", [128, NB, N], F32, ah + 56416)
        self.bias1 = at("gcn_bias", [128, 2, D], F32, bias)
        self.diag = at("mask_diagonal", [128, BP], F32, ah + 68928)

        self.feat = at("features", [128, 1028 * NB], F32, ah + 15360)
        self.resid = at("residual_product", [128, NB, HID], F32, ah + 35936)
        self.prob = at("probs", [128, 5, N], F32, ah + 56416)
        self.score = at("scores", [128, 3, N], F32, ah + 68928)
        self.rows = at("score_rows", [128, 2, 2 * N], F32, ah + 76448)
        self.mask_loop = at("mask_loops", [128, NB, N], BF16, ah + 86464)
        self.mask_plain = at("mask_plain", [128, NB, N], BF16, ah + 92736)
        self.cnt_loop = at("counts_loops", [128, NB, N], I16, bias)
        self.par = [at("par0", [128, HID], F32, h), at("par1", [128, HID], F32, tail),
                    at("par2", [128, HID], F32, ah + 56416 + 7520), at("par3", [128, HID], F32, x + 40000)]
        self.par0b = at("par0b", [128, D], F32, h + 3072)
        self.xh8 = at("x8T_hi", [128, K8, N], F32R, x)
        self.xl8 = at("x8T_lo", [128, K8, N], F32R, x + 20000)
        cols = small + 512
        (self.al_src, self.al_dst, self.al_src2, self.al_max, self.row1, self.row2, self.al_sum) = (
            at(n, [128, NB, HEADS3], F32, cols + 160 * i) for i, n in enumerate(
                ("al_src", "al_dst", "al_src_slope", "al_max", "row_steep", "row_flat", "al_sum")))
        self.z = at("z", [128, NB, 4], F32, cols + 160 * 7)
        self.shift = at("ln_shift", [128, NB], F32, cols + 160 * 7 + 96)
        self.flat = [at("flat0", [128, 2, N], F32, x + 30016), at("flat1", [128, 2, N], F32, ah + 30912)]
        self.al_rows = at("al_rows", [128, HEADS3 - 2, N], F32, x + 30016)
        self.max_scratch = at("max_scratch", [128, N], F32, bias + 6272)


def program(nc, x, src, dst, etype, weights, rgcn_bias, gcn_bias, vec, out):
    ctx = ExitStack()
    with ctx:
        nc.disable_value_cache = True
        mem = Memory(nc)
        ps = ctx.enter_context(nc.psum_tensor("psum", [128, 8 * 512], F32))

        def sem(name):
            return ctx.enter_context(nc.semaphore(name))

        consts_ready = sem("consts_ready")
        edges_loaded = sem("edges_loaded")
        x_loaded = sem("x_loaded")
        bias_loaded = sem("bias_loaded")
        edges_ready = sem("edges_ready")
        onehot_ready = sem("onehot_ready")
        onehot_used = sem("onehot_used")
        sweep_done = sem("sweep_done")
        sweep_read = sem("sweep_read")
        decoded = sem("decoded")
        zeroed = sem("zeroed")
        ctot_begun = sem("ctot_begun")
        degree_done = sem("degree_done")
        inv_ready = sem("inv_ready")
        adj_scaled = sem("adj_scaled")
        adj_hi_ready = sem("adj_hi_ready")
        adj_lo_ready = sem("adj_lo_ready")
        raw_loaded = [sem(f"raw_loaded{i}") for i in range(RAW)]
        w_hi_ready = sem("w_hi_ready")
        w_lo_ready = sem("w_lo_ready")
        w_used = sem("w_used")
        pool_turn = sem("pool_turn")
        turned = sem("turned")
        xT_hi_ready = sem("xT_hi_ready")
        xT_lo_ready = sem("xT_lo_ready")
        h_done = sem("h_done")
        h_hi_ready = sem("h_hi_ready")
        h_lo_ready = sem("h_lo_ready")
        agg_used = sem("agg_used")
        out_done = sem("out_done")
        out_read = sem("out_read")
        vchain = sem("vchain")
        res_loaded = sem("res_loaded")
        stored = sem("stored")
        var_ready = [sem(f"var_ready{n}") for n in range(6)]
        std_ready = [sem(f"std_ready{n}") for n in range(6)]
        shift_ready = [sem(f"shift_ready{n}") for n in range(6)]
        normed = [sem(f"normed{n}") for n in range(6)]
        res_biased = sem("res_biased")
        gained = sem("gained")
        loops_added = sem("loops_added")
        gcn_hi_ready = sem("gcn_hi_ready")
        gcn_lo_ready = sem("gcn_lo_ready")
        counts_kept = sem("counts_kept")
        gdeg_done = sem("gdeg_done")
        gdeg_ready = sem("gdeg_ready")
        gsqrt_ready = sem("gsqrt_ready")
        dinv_ready = sem("dinv_ready")

        UNITS = 2 * NB
        T_L1 = UNITS * (1 + RLAYERS)
        H_LAYER = 2 * NREL * NB
        H_L1 = RLAYERS * H_LAYER
        TAIL = N - 512
        SWEEP_BANKS = [(5, 512, N), (6, 512, N)] + [(m, 0, 512) for m in range(NB)]
        XRES_AT, BIAS1_AT = 175, 190
        FIRST_PREP = 14
        MASK_HALVES = ((0, 3 * BP), (3 * BP, N))

        def bank(b, a=0, e=512, p=BP):
            return ps[0:p, b * 512 + a:b * 512 + e]

        def rows(t, m, a, e):
            return t[0:BP, m, a:e]

        def nodes(m):
            return slice(m * BP, (m + 1) * BP)

        def unit(k, m, i):
            return [(c, m) for c in range(i * (k // 2), (i + 1) * (k // 2))]

        def unit_out(t, u):
            return t[:, u[0][0]:u[-1][0] + 1, nodes(u[0][1])]

        def unit_in(b, u):
            return ps[:, b * 512:b * 512 + len(u) * BP].rearrange("p (c n) -> p c n", c=len(u))

        def unit_bank(m, i):
            return 5 + (2 * m + i) % 3

        block = ctx.enter_context(nc.Block())

        gemm_done = sem("gemm_done")
        gemm_read = sem("gemm_read")
        params_loaded = sem("params_loaded")
        al_ready = sem("al_ready")
        max_row_done = sem("max_row_done")
        max_done = sem("max_done")
        al_row_done = sem("al_row_done")
        al_row_stored = sem("al_row_stored")
        top_ready = sem("top_ready")
        cols_ready = sem("cols_ready")
        rows_done = sem("rows_done")
        rows_read = sem("rows_read")
        exp_done = sem("exp_done")
        prob_ready = sem("prob_ready")
        prob_used = sem("prob_used")
        part_done = sem("part_done")
        part_read = sem("part_read")
        bias_added = sem("bias_added")
        mask_done = sem("mask_done")
        mask_read = sem("mask_read")
        layer_ready = sem("layer_ready")
        elu_in = sem("elu_in")
        elu_out = sem("elu_out")

        T_Q = [T_L1 + (1 + i) * UNITS for i in range(4)]

        def score_pieces(off):
            for m in range(NB):
                a, e = off + m * BP, off + (m + 1) * BP
                cut = -(-(a + 1) // 512) * 512
                for p, q in ((a, min(e, cut)), (cut, e)):
                    if q > p:
                        yield m, p, q, p - a, q - a

        def feat(q, m, h0=0, h1=None):
            v = mem.feat[0:BP, 0:NB * q.heads * q.w].rearrange("p (m h w) -> p m h w", m=NB, h=q.heads)
            return v[:, m, h0:q.heads if h1 is None else h1, 0:q.c]

        def feat_flat(q, m, a, e):
            v = mem.feat[0:BP, 0:NB * q.heads * q.w].rearrange("p (m n) -> p m n", m=NB)
            return v[:, m, a:e]

        def features_of(q, piece):
            a, width = piece
            h, out = a // q.c, []
            while h * q.c < a + width:
                p, e = max(a, h * q.c), min(a + width, (h + 1) * q.c)
                out.append((h, p - h * q.c, e - h * q.c, p - a))
                h += 1
            return out

        def blocks_at(step):
            t = [0, 1] if step == 0 else [step + 1] if step + 1 < (NREL - 1) * NB else []
            return [(1 + i // NB, i % NB) for i in t]

        def in_steps(*stages):
            for step in range(NB + max(lag for _, lag in stages)):
                for stage, lag in stages:
                    if 0 <= step - lag < NB:
                        stage(step - lag)

        @block.sync
        def _(sp):
            for i, v in enumerate((src, dst, etype)):
                sp.dma_start(mem.edges_i[0:BP, i, :], v.rearrange("(p t) -> p t", t=ET)).then_inc(edges_loaded, 16)
            sp.dma_start(mem.xn[0:BP, :, :], x.rearrange("(m p) d -> p m d", p=BP)).then_inc(x_loaded, 16)
            sp.dma_start(mem.bias0[0:BP, :, :].rearrange("p l d -> p (l d)"),
                         rgcn_bias.rearrange("(a l) d -> a (l d)", a=1).to_broadcast([BP, RLAYERS * D])
                         ).then_inc(bias_loaded, 16)

            def load(c, slot, first=False):
                if not first:
                    sp.wait_ge(w_lo_ready, c - RAW + 1)
                sp.dma_start(mem.raw[:, slot, :], weights[bass.ds(c, 1), :, :].rearrange("a p n -> p (a n)")
                             ).then_inc(raw_loaded[slot], 16)

            for c in range(RAW):
                load(c, c, first=True)
            with sp.Fori(1, XRES_AT // RAW) as i:
                for slot in range(RAW):
                    load(i * RAW + slot, slot)
            sp.wait_ge(agg_used, (2 * RLAYERS - 1) * (NREL * NB - 1) + 2 * NB)
            sp.dma_start(mem.xres[0:BP, :, :], x.rearrange("(m p) d -> p m d", p=BP)).then_inc(res_loaded, 16)
            with sp.Fori(XRES_AT // RAW, BIAS1_AT // RAW) as i:
                for slot in range(RAW):
                    load(i * RAW + slot, slot)
            sp.wait_ge(out_read, 10 * RLAYERS)
            sp.dma_start(mem.bias1[0:BP, :, :].rearrange("p l d -> p (l d)"),
                         gcn_bias.rearrange("(a l) d -> a (l d)", a=1).to_broadcast([BP, 2 * D])
                         ).then_inc(bias_loaded, 16)
            with sp.Fori(BIAS1_AT // RAW, NCHUNKS // RAW) as i:
                for slot in range(RAW):
                    load(i * RAW + slot, slot)
            for c in range(NCHUNKS // RAW * RAW, NCHUNKS):
                load(c, c % RAW)
            o = out.rearrange("(m p) d -> p m d", p=BP)
            for m in range(NB):
                sp.wait_ge(normed[5], m + 1)
                sp.dma_start(o[:, m, :], mem.xres[0:BP, m, :]).then_inc(stored, 16)
            sp.wait_ge(stored, 16 * NB)

        @block.gpsimd
        def _(pool):
            nc.gpsimd.memset(mem.ones[:, :], 1.0)
            nc.gpsimd.iota(mem.iota[:, :], pattern=[[1, N]], base=0, channel_multiplier=0,
                           allow_small_or_imprecise_dtypes=True)
            nc.gpsimd.memset(mem.ident[:, :], 0.0).then_inc(consts_ready, 1)
            pool.wait_ge(consts_ready, 1)
            nc.gpsimd.affine_select(out=mem.ident[:, :], in_=mem.ident[:, :], compare_op=ALU.not_equal, fill=1.0,
                                    base=0, pattern=[[-1, 128]], channel_multiplier=1).then_inc(consts_ready, 1)
            nc.gpsimd.memset(mem.sweep[:, 1, :, :], 0).then_inc(decoded, 1)
            for r in (2, 3, 0, 1):
                nc.gpsimd.memset(mem.cnt[:, r, :, :], 0.0).then_inc(zeroed, 1)

            def split(c, slot, raw_slot, turn, first=False):
                if not first:
                    pool.wait_ge(w_used, c - WRING + 1)
                pool.wait_ge(raw_loaded[raw_slot], 16 * turn)
                pool.sem_inc(pool_turn, 1)
                nc.gpsimd.tensor_copy(mem.wh[:, slot, :], mem.raw[:, raw_slot, :]).then_inc(w_hi_ready, 1)
                pool.wait_ge(w_hi_ready, c + 1)
                nc.gpsimd.tensor_tensor(mem.wl[:, slot, :], mem.raw[:, raw_slot, :],
                                        mem.wh[:, slot, :].bitcast(F32), ALU.subtract).then_inc(w_lo_ready, 1)

            for c in range(WRING):
                split(c, c, c % RAW, c // RAW + 1, first=True)
            def split_loop(c0, c1):
                with pool.Fori(c0 // WRING, c1 // WRING) as i:
                    for j in range(WRING):
                        split(i * WRING + j, j, j % RAW, i * (WRING // RAW) + j // RAW + 1)

            def split_lo(c0, c1):
                for c in range(c0, c1):
                    pool.wait_ge(w_hi_ready, c + 1)
                    nc.gpsimd.tensor_tensor(mem.wl[:, c % WRING, :], mem.raw[:, c % RAW, :],
                                            mem.wh[:, c % WRING, :].bitcast(F32), ALU.subtract).then_inc(w_lo_ready, 1)

            split_loop(WRING, ACT_SPLITS)
            split_lo(ACT_SPLITS, Q0.end + AHEAD)
            pool.wait_ge(gemm_read, Q0.gemm0 + len(Q0.banks))
            pool.wait_ge(params_loaded, 16 * 4)
            for m in range(NB):
                r = mem.resid[0:BP, m, :]
                nc.gpsimd.tensor_tensor(r, r, mem.par[3][0:BP, :], ALU.add).then_inc(bias_added, 1)
            for m in range(NB):
                pool.wait_ge(normed[2], m + 1)
                g = mem.par[1][0:BP, :].rearrange("p (h c) -> p h c", h=HEADS2)
                nc.gpsimd.tensor_tensor(feat(Q0, m), feat(Q0, m), g, ALU.mult).then_inc(gained, 1)
            split_lo(Q0.end + AHEAD, Q1.end + AHEAD)
            pool.wait_ge(gemm_read, Q1.gemm0 + len(Q1.banks))
            pool.wait_ge(params_loaded, 16 * (6 + 6))
            for m in range(NB):
                r = mem.resid[0:BP, m, 0:D]
                nc.gpsimd.tensor_tensor(r, r, mem.par[3][0:BP, 0:D], ALU.add).then_inc(bias_added, 1)
                pool.wait_ge(bias_added, NB + 3 * m + 1)
                nc.gpsimd.tensor_tensor(r, r, mem.xres[0:BP, m, :], ALU.add).then_inc(bias_added, 1)
                pool.wait_ge(bias_added, NB + 3 * m + 2)
                nc.gpsimd.tensor_tensor(r, r, mem.par0b[0:BP, :], ALU.add).then_inc(bias_added, 1)
            for m in range(NB):
                pool.wait_ge(normed[3], m + 1)
                t = feat_flat(Q1, m, 0, D)
                nc.gpsimd.tensor_tensor(t, t, mem.par[0][0:BP, 0:D], ALU.mult).then_inc(gained, 1)
            split_lo(Q1.end + AHEAD, Q2.end + AHEAD)
            split_lo(Q2.end + AHEAD, NCHUNKS)
            pool.wait_ge(params_loaded, 16 * 18)
            for m in range(NB):
                r = mem.xres[0:BP, m, :]
                nc.gpsimd.tensor_tensor(r, r, mem.par[1][0:BP, 0:D], ALU.add).then_inc(res_biased, 1)

        @block.scalar
        def _(act):
            def turn_hi(u0, k, dst_hi, func, m):
                for i in range(2):
                    act.wait_ge(turned, u0 + (2 * m + i + 1))
                    u = unit(k, m, i)
                    nc.scalar.activation(unit_out(dst_hi, u), unit_in(unit_bank(m, i), u), func
                                         ).then_inc(xT_hi_ready, 1)

            def read_sweep(done, free, s):
                for j, (b, a, e) in enumerate(SWEEP_BANKS):
                    act.wait_ge(sweep_done, done + j + 1)
                    if j == 0:
                        act.wait_ge(decoded, free + 1)
                    if b == 5:
                        o, i = mem.sweep[0:BP, s, 0:4, 512:N], bank(5, 0, 4 * TAIL).rearrange("p (m n) -> p m n", m=4)
                    elif b == 6:
                        o, i = mem.sweep[0:BP, s, 4, 512:N], bank(6, 0, TAIL)
                    else:
                        o, i = mem.sweep[0:BP, s, b, 0:512], bank(b)
                    nc.scalar.activation(o, i, ACT.Copy).then_inc(sweep_read, 1)

            def h_hi(i, slot, scale=None):
                act.wait_ge(h_done, i + 1)
                if scale is None:
                    nc.scalar.activation(mem.hh[0:BP, slot, :], bank(5 + slot, 0, HW), ACT.Copy
                                         ).then_inc(h_hi_ready, 1)
                else:
                    nc.scalar.activation(mem.hh[0:BP, slot, :], bank(5 + slot, 0, HW), ACT.Copy, scale=scale
                                         ).then_inc(h_hi_ready, 1)

            for m in range(NB):
                turn_hi(0, KC, mem.xh, ACT.Copy, m)
            act.sem_inc(sweep_read, 1)
            with act.Fori(0, CHUNKS) as c:
                read_sweep(c * 14, c * 40, 0)
                read_sweep(c * 14 + 7, c * 40 + 20, 1)
            act.wait_ge(decoded, CHUNKS * 40 + 20 + 1)
            nc.scalar.activation(mem.ctot[0:BP, :, :], mem.cnt[0:BP, 0, :, :], ACT.Copy).then_inc(ctot_begun, 1)

            def adjacency_hi(r, m):
                act.wait_ge(adj_scaled, r * NB + m + 1)
                nc.scalar.activation(mem.ah[0:BP, r, m, :], mem.cnt[0:BP, r, m, :], ACT.Copy).then_inc(adj_hi_ready, 1)

            for m in range(NB):
                adjacency_hi(0, m)
            for i in range(H_LAYER // 2):
                h_hi(i, i % 2)
                for r, m in blocks_at(i):
                    adjacency_hi(r, m)
            for i in range(H_LAYER // 2, H_LAYER):
                h_hi(i, i % 2)
            for m in range(NB):
                turn_hi(UNITS, KC, mem.xh, ACT.Relu, m)
            with act.Fori(1, RLAYERS - 1) as l:
                for i in range(H_LAYER):
                    h_hi(l * H_LAYER + i, i % 2)
                for m in range(NB):
                    turn_hi(l * UNITS + UNITS, KC, mem.xh, ACT.Relu, m)
            for i in range(H_LAYER):
                h_hi((RLAYERS - 1) * H_LAYER + i, i % 2)

            def std(n):
                def stage(m):
                    act.wait_ge(var_ready[n], m + 1)
                    t = mem.std[0:BP, m:m + 1]
                    nc.scalar.activation(t, t, ACT.Sqrt).then_inc(std_ready[n], 1)
                return stage

            def norm(n, source, dest):
                def stage(m):
                    act.wait_ge(shift_ready[n], m + 1)
                    nc.scalar.activation(dest(m), source(m), ACT.Identity, bias=mem.shift[0:BP, m:m + 1],
                                         scale=mem.std[0:BP, m:m + 1]).then_inc(normed[n], 1)
                return stage

            def hi(t, k, dst, func=ACT.Copy):
                return lambda m: turn_hi(t, k, dst, func, m)

            def x_nat(m):
                return mem.xn[0:BP, m, :]

            def x_res(m):
                return mem.xres[0:BP, m, :]

            def gcn_hi(m):
                if m == 0:
                    act.wait_ge(out_read, RLAYERS * 10)
                nc.scalar.activation(mem.ch[0:BP, m, :], mem.cf[0:BP, m, :], ACT.Copy).then_inc(gcn_hi_ready, 1)

            def degree_root(m):
                if m == 0:
                    act.wait_ge(gdeg_ready, 1)
                    nc.scalar.activation(mem.deg[0:BP, :], mem.deg[0:BP, :], ACT.Sqrt).then_inc(gsqrt_ready, 1)

            in_steps((std(0), 0), (norm(0, x_nat, x_res), 1), (hi(T_L1 - UNITS, KC, mem.xh), 2), (gcn_hi, 3), (degree_root, 6))
            act.wait_ge(dinv_ready, 1)
            for layer in range(2):
                for i in range(2 * NB):
                    h_hi(H_L1 + layer * 2 * NB + i, i % 2, mem.dinv[0:BP, i % NB:i % NB + 1])
                if layer == 0:
                    for m in range(NB):
                        turn_hi(T_L1, KC, mem.xh, ACT.Relu, m)

            def load_row(name, row, width):
                act.dma_start(row[0:BP, 0:width],
                              vec[name].rearrange("(a n) -> a n", a=1).to_broadcast([BP, width])
                              ).then_inc(params_loaded, 16)

            chunks_split = [ACT_SPLITS]

            def split_hi(end):
                for c in range(chunks_split[0], min(end, NCHUNKS)):
                    act.wait_ge(raw_loaded[c % RAW], 16 * (c // RAW + 1))
                    act.wait_ge(w_used, c - WRING + 1)
                    nc.scalar.activation(mem.wh[:, c % WRING, :], mem.raw[:, c % RAW, :], ACT.Copy
                                         ).then_inc(w_hi_ready, 1)
                chunks_split[0] = max(chunks_split[0], min(end, NCHUNKS))

            def attention(q, later):
                n = len(q.pieces)

                flat = mem.flat[0 if q.index == 0 else 1]

                def read_rows(h):
                    act.wait_ge(rows_done, q.head0 + h + 1)
                    if h >= 2:
                        act.wait_ge(exp_done, 2 * (q.head0 + h - 1) * NB)
                    a = q.rows_col(h)
                    nc.scalar.activation(mem.rows[0:BP, h % 2, :], ps[0:BP, a:a + 2 * N], ACT.Copy
                                         ).then_inc(rows_read, 1)

                def exps(j):
                    h, k = j // NB, j % NB
                    if k == 0:
                        act.wait_ge(rows_read, q.head0 + h + 1)
                        act.wait_ge(cols_ready, q.head0 + h + 1)
                    if j >= 3:
                        act.wait_ge(prob_ready, q.head0 * NB + j - 2)
                    nc.scalar.activation(mem.score[0:BP, j % 3, :], mem.rows[0:BP, h % 2, 0:N], ACT.Exp,
                                         bias=mem.al_src[0:BP, k, h:h + 1]).then_inc(exp_done, 1)
                    if j >= 2:
                        act.wait_ge(top_ready, q.head0 * NB + j - 1)
                    nc.scalar.activation(flat[0:BP, j % 2, :], mem.rows[0:BP, h % 2, N:2 * N], ACT.Exp,
                                         bias=mem.al_src2[0:BP, k, h:h + 1]).then_inc(exp_done, 1)

                for g, bank_ in enumerate(q.banks):
                    piece, m = g // NB, g % NB
                    if m == (NB - 1 if piece == 0 else 0):
                        split_hi(q.chunk + (piece + 1) * q.k + 4)
                    act.wait_ge(gemm_done, q.gemm0 + g + 1)
                    a, width = q.pieces[piece % n]
                    b = bank(bank_, 0, width)
                    if piece >= n:
                        ins = nc.scalar.activation(mem.resid[0:BP, m, a:a + width], b, ACT.Copy)
                    elif a % q.c == 0 and width % q.c == 0:
                        ins = nc.scalar.activation(feat(q, m, a // q.c, (a + width) // q.c),
                                                   b.rearrange("p (h c) -> p h c", c=q.c), ACT.Copy)
                    else:
                        for h, p, e, off in features_of(q, (a, width)):
                            ins = nc.scalar.activation(feat_flat(q, m, h * q.w + p, h * q.w + e),
                                                       b[:, off:off + e - p], ACT.Copy)
                    ins.then_inc(gemm_read, 1)
                    if m == NB - 1 and piece == n:
                        act.wait_ge(al_ready, q.al0 + q.heads * q.al_head)
                        for args in later:
                            load_row(*args)
                    if m == NB - 1 and (piece, q.index) in READ_ROWS:
                        read_rows(READ_ROWS[piece, q.index])
                    if q.residual and g == len(q.banks) - NB - 1:
                        for j in range(3):
                            exps(j)
                if not q.residual:
                    read_rows(0)
                if q.stored:
                    exps(0)
                    exps(1)
                    for h in range(q.first, q.heads):
                        act.wait_ge(al_row_done, h - q.first + 1)
                        a = h % 2 * 1024
                        nc.scalar.activation(mem.al_rows[0:BP, h - q.first, :], ps[0:BP, a:a + N], ACT.Copy
                                             ).then_inc(al_row_stored, 1)
                for j in range(3 if q.residual else 2 if q.stored else 0, q.heads * NB):
                    h, k = j // NB, j % NB
                    split_hi(min(chunks_split[0] + 2, q.end + AHEAD))
                    exps(j)
                    if k == 3 and h + 1 < q.heads and h + 1 not in q.rows_at.values():
                        read_rows(h + 1)
                split_hi(q.end + AHEAD)

            par = mem.par

            act.wait_ge(out_done, RLAYERS * 10 + 4 * NB)
            for args in (("L2_gnn_a_src1", par[0], HID), ("L2_gnn_a_dst1", par[1], HID)):
                load_row(*args)
            in_steps((std(1), 0), (norm(1, x_nat, x_res), 1), (hi(T_Q[0], KC, mem.xh), 2))
            act.wait_ge(counts_kept, 1)
            for args in (("L2_gnn_be1", par[2], HID), ("L2_gnn_br1", par[3], HID)):
                load_row(*args)
            attention(Q0, [("L2_gnn_b1", par[0], HID), ("L2_gnn_g1", par[1], HID)])
            in_steps((std(2), 0), (norm(2, lambda m: feat(Q0, m), lambda m: feat(Q0, m)), 1),
                     (hi(T_Q[1], K8, mem.xh8), 4))
            act.wait_ge(layer_ready, NB)
            act.wait_ge(bias_added, NB)
            for args in (("L2_gnn_a_src2", par[0], D), ("L2_gnn_a_dst2", mem.par0b, D),
                         ("L2_gnn_b2", par[1], D), ("L2_gnn_br2", par[3], D)):
                load_row(*args)
            attention(Q1, [("L2_gnn_g2", par[0], D), ("L2_gnn_be2", mem.par0b, D)])

            def q1_out(m):
                return feat_flat(Q1, m, 0, D)

            in_steps((std(3), 0), (norm(3, q1_out, q1_out), 1), (std(4), 3), (norm(4, q1_out, x_res), 4),
                     (hi(T_Q[2], KC, mem.xh), 5))
            for args in (("L3_gnn_a_src1", par[0], D), ("L3_gnn_a_dst1", mem.par0b, D), ("L3_gnn_b1", par[1], D)):
                load_row(*args)
            attention(Q2, [])

            def elu_exp(m):
                act.wait_ge(part_read, (Q2.group0 + 1) * NB + m + 1)
                nc.scalar.activation(mem.feat[0:BP, m * D:(m + 1) * D], mem.resid[0:BP, m, 0:D], ACT.Exp
                                     ).then_inc(elu_out, 1)

            in_steps((elu_exp, 0), (hi(T_Q[3], KC, mem.xh), 2))
            for args in (("L3_gnn_a_src2", par[0], D), ("L3_gnn_a_dst2", mem.par0b, D), ("L3_gnn_b2", par[1], D)):
                load_row(*args)
            attention(Q3, [])
            in_steps((std(5), 0), (norm(5, x_nat, x_res), 1))

        @block.vector
        def _(dve):
            steps = [0]

            def link(ins):
                steps[0] += 1
                ins.then_inc(vchain, 1)
                dve.wait_ge(vchain, steps[0])

            def turn_lo(u0, k, dst_hi, dst_lo, relu, m):
                for i in range(2):
                    dve.wait_ge(xT_hi_ready, u0 + (2 * m + i + 1))
                    u = unit(k, m, i)
                    o, i_, h = unit_out(dst_lo, u), unit_in(unit_bank(m, i), u), unit_out(dst_hi, u).bitcast(F32)
                    if relu:
                        ins = nc.vector.scalar_tensor_tensor(o, i_, 0.0, h, ALU.max, ALU.subtract)
                    else:
                        ins = nc.vector.tensor_tensor(o, i_, h, ALU.subtract)
                    ins.then_inc(xT_lo_ready, 1)

            dve.wait_ge(edges_loaded, 48)
            for t in (mem.src_f, mem.dst_f, mem.typ_f):
                ins = nc.vector.memset(t[:, :], -1.0)
            link(ins)
            for i, t in enumerate((mem.src_f, mem.dst_f, mem.typ_f)):
                ins = nc.vector.tensor_copy(t[0:BP, 0:ET], mem.edges_i[0:BP, i, :])
            link(ins)
            link(nc.vector.tensor_scalar(mem.tmp_f[0:BP, :], mem.typ_f[0:BP, :], 1.0, None, ALU.is_equal))
            link(nc.vector.scalar_tensor_tensor(mem.val_f[0:BP, :], mem.typ_f[0:BP, :], 3.0, mem.tmp_f[0:BP, :],
                                                ALU.is_equal, ALU.add))
            link(nc.vector.tensor_scalar(mem.val_f[0:BP, :], mem.val_f[0:BP, :], PAIR_BASE - 1.0, 1.0, ALU.mult, ALU.add))
            link(nc.vector.tensor_scalar(mem.dst_f[0:BP, :], mem.dst_f[0:BP, :], 1.0, None, ALU.add))
            for p, op in enumerate((ALU.is_lt, ALU.is_ge)):
                link(nc.vector.scalar_tensor_tensor(mem.dstp_f[0:BP, p, :], mem.typ_f[0:BP, :], 2.0,
                                                    mem.dst_f[0:BP, :], op, ALU.mult))
                link(nc.vector.tensor_scalar(mem.dstp_f[0:BP, p, :], mem.dstp_f[0:BP, p, :], 1.0, None, ALU.subtract))
            dve.wait_ge(consts_ready, 2)
            for m in range(NB):
                turn_lo(0, KC, mem.xh, mem.xl, False, m)

            def decode(s, k, before):
                m, step = k // 4, k % 4
                odd = mem.odd[0:BP, m % 2, :]
                both = mem.sweep[0:BP, s, m, :]
                if step == 0:
                    ins = nc.vector.tensor_scalar(odd, both, 12, None, ALU.logical_shift_right)
                elif step == 1:
                    ins = nc.vector.tensor_scalar(both, both, PAIR_BASE - 1, None, ALU.bitwise_and)
                elif step == 2:
                    dve.wait_ge(decoded, before)
                    c = mem.cnt[0:BP, 2 * s + 1, m, :]
                    ins = nc.vector.tensor_tensor(c, c, odd, ALU.add)
                else:
                    dve.wait_ge(decoded, before)
                    c = mem.cnt[0:BP, 2 * s, m, :]
                    ins = nc.vector.tensor_tensor(c, c, both, ALU.add)
                return ins.then_inc(decoded, 1)

            with dve.Fori(0, CHUNKS) as c:
                for p in range(2):
                    for t in range(SWEEP):
                        n, slot = p * SWEEP + t, (p * SWEEP + t) % OH_RING
                        dve.wait_ge(onehot_used, c * (2 * SWEEP) + (n + 1))
                        col = bass.ds(c * SWEEP + t, 1)
                        nc.vector.tensor_scalar(mem.oh_src[0:BP, slot, :], mem.iota[0:BP, :], mem.src_f[0:BP, col],
                                                mem.val_f[0:BP, col], ALU.is_equal, ALU.mult)
                        nc.vector.tensor_scalar(mem.oh_dst[0:BP, slot, :], mem.iota[0:BP, :], mem.dstp_f[0:BP, p, col],
                                                None, ALU.is_equal).then_inc(onehot_ready, 1)
                        if 2 <= t < 22:
                            if t == 2:
                                dve.wait_ge(zeroed, 2 * p + 2)
                                dve.wait_ge(sweep_read, c * 14 + 7 * p + 1)
                            decode(1 - p, t - 2, c * 40 + (20 * p + t - 2))
            dve.wait_ge(sweep_read, CHUNKS * 14 + 1)
            for k in range(20):
                decode(1, k, CHUNKS * 40 + k)

            def row3(ap):
                return ap.unsqueeze(1).to_broadcast([BP, NB, N])

            dve.wait_ge(decoded, CHUNKS * 40 + 20 + 1)
            for r in range(NREL):
                dve.wait_ge(degree_done, r + 1)
                nc.vector.tensor_scalar(mem.inv[r][0:BP, :], ps[0:BP, r * 1024:r * 1024 + N], 1.0, None, ALU.max
                                        ).then_inc(inv_ready, 1)
            dve.wait_ge(inv_ready, NREL)

            def inverse(r, a=0, e=N):
                inv = mem.inv[r][0:BP, a:e]
                link(nc.vector.reciprocal(inv, inv))

            def scale(r, m):
                c = mem.cnt[0:BP, r, m, :]
                if r:
                    link(nc.vector.tensor_tensor(mem.ctot[0:BP, m, :], mem.ctot[0:BP, m, :], c, ALU.add))
                nc.vector.tensor_tensor(c, c, mem.inv[r][0:BP, :], ALU.mult).then_inc(adj_scaled, 1)

            def adjacency_lo(r, m):
                dve.wait_ge(adj_hi_ready, r * NB + m + 1)
                nc.vector.tensor_tensor(mem.al[0:BP, r, m, :], mem.cnt[0:BP, r, m, :],
                                        mem.ah[0:BP, r, m, :].bitcast(F32), ALU.subtract).then_inc(adj_lo_ready, 1)

            inverse(0)
            dve.wait_ge(ctot_begun, 1)
            for m in range(NB):
                scale(0, m)
            inverse(1)
            for m in range(NB):
                adjacency_lo(0, m)
            inverse(2)

            def h_lo(i, slot, scale=None):
                dve.wait_ge(h_hi_ready, i + 1)
                o, p, h = mem.hl[0:BP, slot, :], bank(5 + slot, 0, HW), mem.hh[0:BP, slot, :].bitcast(F32)
                if scale is None:
                    nc.vector.tensor_tensor(o, p, h, ALU.subtract).then_inc(h_lo_ready, 1)
                else:
                    nc.vector.scalar_tensor_tensor(o, p, scale, h, ALU.mult, ALU.subtract).then_inc(h_lo_ready, 1)

            def x_nat(m, a=0, e=D):
                return mem.xn[0:BP, m, a:e]

            def x_res(m, a=0, e=D):
                return mem.xres[0:BP, m, a:e]

            def stat(m, f, source):
                return nc.vector.bn_stats(mem.stats[0:BP, m, f, :], source)

            def var(n, m):
                link(nc.vector.bn_aggr(mem.mv[0:BP, m, :], mem.stats[0:BP, m, :, :]))
                nc.vector.tensor_scalar(mem.std[0:BP, m:m + 1], mem.mv[0:BP, m, 1:2], LN_EPS, None, ALU.add
                                        ).then_inc(var_ready[n], 1)

            def shift(n):
                def stage(m):
                    dve.wait_ge(std_ready[n], m + 1)
                    t = mem.std[0:BP, m:m + 1]
                    link(nc.vector.reciprocal(t, t))
                    nc.vector.scalar_tensor_tensor(mem.shift[0:BP, m:m + 1], mem.mv[0:BP, m, 0:1], -1.0, t,
                                                   ALU.mult, ALU.mult).then_inc(shift_ready[n], 1)
                return stage

            def lo(t, k=KC, relu=False):
                dst = (mem.xh, mem.xl) if k == KC else (mem.xh8, mem.xl8)
                return lambda m: turn_lo(t, k, *dst, relu, m)

            def res_first_half(m, bias_row):
                link(nc.vector.tensor_tensor(x_nat(m, 0, HW), x_nat(m, 0, HW), x_res(m, 0, HW), ALU.add))
                stat(m, 0, x_nat(m, 0, HW))
                link(nc.vector.tensor_tensor(x_res(m, HW), x_res(m, HW), bias_row, ALU.add))

            dve.wait_ge(bias_loaded, 16)

            def rgcn_sums(l, f):
                def stage(m):
                    dve.wait_ge(out_done, l * 10 + (f * NB + m + 1))
                    nc.vector.tensor_tensor(mem.xn[0:BP, m:m + 1, f * HW:(f + 1) * HW], bank(m, 0, HW).unsqueeze(1),
                                            mem.bias0[0:BP, bass.ds(l, 1), f * HW:(f + 1) * HW], ALU.add
                                            ).then_inc(out_read, 1)
                return stage

            def second_half(l):
                for i in range(H_LAYER // 2, H_LAYER):
                    h_lo(l * H_LAYER + i, i % 2)
                in_steps((rgcn_sums(l, 1), 0), (lo(l * UNITS + UNITS, relu=True), 2))

            waiting = []
            for i in range(H_LAYER // 2):
                h_lo(i, i % 2)
                for r, m in waiting:
                    adjacency_lo(r, m)
                waiting = blocks_at(i)
                for r, m in waiting:
                    scale(r, m)
                if i < NB:
                    inverse(NREL - 1, i * BP, (i + 1) * BP)
            for m in range(NB):
                rgcn_sums(0, 0)(m)
            second_half(0)
            with dve.Fori(1, RLAYERS - 1) as l:
                for i in range(H_LAYER // 2):
                    h_lo(l * H_LAYER + i, i % 2)
                for m in range(NB):
                    rgcn_sums(l, 0)(m)
                second_half(l)
            l = RLAYERS - 1
            for i in range(H_LAYER // 2):
                h_lo(l * H_LAYER + i, i % 2)
            for m in range(NB):
                dve.wait_ge(out_done, l * 10 + (m + 1))
                nc.vector.tensor_tensor(x_nat(m, 0, HW), bank(m, 0, HW), mem.bias0[0:BP, l, 0:HW], ALU.add
                                        ).then_inc(out_read, 1)
            for i in range(H_LAYER // 2):
                h_lo(l * H_LAYER + H_LAYER // 2 + i, i % 2)
                if FIRST_PREP <= i < FIRST_PREP + NB:
                    dve.wait_ge(out_read, l * 10 + NB)
                    dve.wait_ge(res_loaded, 16)
                    m = i - FIRST_PREP
                    res_first_half(m, mem.bias0[0:BP, l, HW:D])
                    link(nc.vector.tensor_copy(mem.cf[0:BP, m, :], mem.ctot[0:BP, m, :]))
                    v = mem.cf[0:BP, m, nodes(m)]
                    nc.vector.tensor_tensor(v, v, mem.ident[0:BP, 0:BP], ALU.add).then_inc(loops_added, 1)

            def rgcn_out(m):
                dve.wait_ge(out_done, l * 10 + (NB + m + 1))
                nc.vector.tensor_tensor(x_nat(m, HW), bank(m, 0, HW), x_res(m, HW), ALU.add).then_inc(out_read, 1)
                dve.wait_ge(out_read, l * 10 + (NB + m + 1))
                link(stat(m, 1, x_nat(m, HW)))
                var(0, m)

            def degrees(m):
                if m == 0:
                    dve.wait_ge(gdeg_done, 1)
                    nc.vector.tensor_copy(mem.deg[0:BP, :], bank(0, 0, NB)).then_inc(gdeg_ready, 1)

            def inverse_root(m):
                if m == 0:
                    dve.wait_ge(gsqrt_ready, 1)
                    nc.vector.reciprocal(mem.dinv[0:BP, :], mem.deg[0:BP, :]).then_inc(dinv_ready, 1)

            def gcn_lo(m):
                dve.wait_ge(gcn_hi_ready, m + 1)
                nc.vector.tensor_tensor(mem.cl[0:BP, m, :], mem.cf[0:BP, m, :], mem.ch[0:BP, m, :].bitcast(F32),
                                        ALU.subtract).then_inc(gcn_lo_ready, 1)

            in_steps((rgcn_out, 0), (shift(0), 1), (lo(T_L1 - UNITS), 3), (gcn_lo, 4), (degrees, 6), (inverse_root, 7))
            dve.wait_ge(dinv_ready, 1)
            dve.wait_ge(bias_loaded, 32)

            def masks(n):
                m, half = n // 2, n % 2
                dve.wait_ge(mask_done, n + 1)
                if n:
                    dve.wait_ge(mask_read, n)
                a, e = MASK_HALVES[half]
                row = bank(7, 0, e - a)
                nc.vector.tensor_scalar(mem.mask_loop[0:BP, m, a:e], row, 0.0, NEG, ALU.is_equal, ALU.mult)
                ins = nc.vector.tensor_scalar(mem.mask_plain[0:BP, m, a:e], row, 0.0, NEG, ALU.is_equal, ALU.mult)
                if a <= m * BP < e:
                    link(ins)
                    link(nc.vector.tensor_tensor(mem.diag[0:BP, :], row[:, m * BP - a:m * BP - a + BP],
                                                 mem.ident[0:BP, 0:BP], ALU.subtract))
                    ins = nc.vector.tensor_scalar(mem.mask_plain[0:BP, m, nodes(m)], mem.diag[0:BP, :], 0.0, NEG,
                                                  ALU.is_equal, ALU.mult)
                ins.then_inc(mask_read, 1)

            def gcn_sums(layer, f, m, plus):
                n = RLAYERS * 10 + (layer * 2 + f) * NB + m + 1
                dve.wait_ge(out_done, n)
                nc.vector.scalar_tensor_tensor(x_nat(m, f * HW, (f + 1) * HW), bank(m, 0, HW), mem.dinv[0:BP, m:m + 1],
                                               plus, ALU.mult, ALU.add).then_inc(out_read, 1)
                return n

            for layer in range(2):
                for f in range(2):
                    for i in range(NB):
                        h_lo(H_L1 + layer * 2 * NB + f * NB + i, (f * NB + i) % 2, mem.dinv[0:BP, i:i + 1])
                        if layer == 0:
                            masks(f * NB + i)
                        if layer == 1 and f == 1:
                            dve.wait_ge(out_read, RLAYERS * 10 + 3 * NB)
                            res_first_half(i, mem.bias1[0:BP, 1, HW:D])
                    if f == 0:
                        for m in range(NB):
                            gcn_sums(layer, f, m, mem.bias1[0:BP, layer, 0:HW])
                    elif layer == 0:
                        in_steps((lambda m: gcn_sums(0, 1, m, mem.bias1[0:BP, 0, HW:D]), 0),
                                 (lo(T_L1, relu=True), 2))

            def gcn_out(m):
                n = gcn_sums(1, 1, m, x_res(m, HW))
                dve.wait_ge(out_read, n)
                link(stat(m, 1, x_nat(m, HW)))
                var(1, m)

            in_steps((gcn_out, 0), (shift(1), 1), (lo(T_Q[0]), 3))
            nc.vector.tensor_copy(mem.cnt_loop[0:BP, :, :], mem.cf[0:BP, :, :]).then_inc(counts_kept, 1)

            def attention(q, bias, src_row, dst_row, dest, first, all_rows, tail, between=None):
                P0 = q.head0 * NB
                mask = mem.mask_loop if q.loops else mem.mask_plain
                cnt = mem.cnt_loop if q.loops else mem.ctot
                flat = mem.flat[0 if q.index == 0 else 1]
                v = mem.feat[0:BP, 0:NB * q.heads * q.w].rearrange("p (h w) -> p h w", w=q.w)
                link(nc.vector.memset(v[:, :, q.c:q.w], 1.0))
                dve.wait_ge(params_loaded, 16 * first)
                scratch = mem.prob[0:BP, 0:3, :].rearrange("p a n -> p (a n)")

                def head_scores(h):
                    c = q.c // q.al_parts
                    n = h * q.al_head
                    for part in range(q.al_parts):
                        end = h * q.c + (part + 1) * c
                        last_piece = next(i for i, (a, w) in enumerate(q.pieces) if end <= a + w)
                        for m in range(NB):
                            dve.wait_ge(gemm_read, q.gemm0 + last_piece * NB + m + 1)
                            for row, o in ((src_row, mem.al_src), (dst_row, mem.al_dst)):
                                if n >= 2:
                                    dve.wait_ge(al_ready, q.al0 + n - 1)
                                a = h * q.w + part * c
                                nc.vector.tensor_tensor_reduce(
                                    out=scratch[:, n % 2 * D:n % 2 * D + c], in0=feat_flat(q, m, a, a + c),
                                    in1=row[0:BP, end - c:end], scale=1.0, scalar=0.0, op0=ALU.mult, op1=ALU.add,
                                    accum_out=o[0:BP, m, h + part:h + part + 1]).then_inc(al_ready, 1)
                                n += 1
                    dve.wait_ge(al_ready, q.al0 + n)
                    if q.al_parts == 2:
                        for o in (mem.al_src, mem.al_dst):
                            nc.vector.tensor_tensor(o[0:BP, :, 0], o[0:BP, :, 0], o[0:BP, :, 1], ALU.add
                                                    ).then_inc(al_ready, 1)
                        dve.wait_ge(al_ready, q.al0 + n + 2)
                    link(nc.vector.tensor_scalar(mem.al_src2[0:BP, :, h], mem.al_src[0:BP, :, h], SLOPE, None,
                                                 ALU.mult))

                def largest(h, m):
                    if q.stored and h >= q.first:
                        row = mem.al_rows[0:BP, h - q.first, :]
                        dve.wait_ge(al_row_stored, h - q.first + 1)
                    else:
                        row = ps[0:BP, q.rows_col(h):q.rows_col(h) + N]
                        if m == 0:
                            dve.wait_ge(max_row_done, q.max_count(h))
                    done = (q.head0 + h) * NB + m
                    if h or m:
                        dve.wait_ge(max_done, done)
                    nc.vector.tensor_tensor_reduce(
                        out=mem.max_scratch[0:BP, :], in0=row, in1=mask[0:BP, m, :], scale=1.0,
                        scalar=-3.0e38, op0=ALU.add, op1=ALU.max, accum_out=mem.al_max[0:BP, m, h:h + 1]
                    ).then_inc(max_done, 1)

                def columns(h):
                    dve.wait_ge(max_done, (q.head0 + h + 1) * NB)
                    u, m_, d = mem.al_sum[0:BP, :, h], mem.al_max[0:BP, :, h], mem.al_dst[0:BP, :, h]
                    link(nc.vector.tensor_tensor(u, m_, d, ALU.add))
                    link(nc.vector.scalar_tensor_tensor(m_, u, SLOPE, u, ALU.mult, ALU.max))
                    nc.vector.tensor_tensor(mem.row1[0:BP, :, h], d, m_, ALU.subtract)
                    nc.vector.scalar_tensor_tensor(mem.row2[0:BP, :, h], d, SLOPE, m_, ALU.mult, ALU.subtract
                                                   ).then_inc(cols_ready, 1)

                def probs(j):
                    dve.wait_ge(top_ready, P0 + j + 1)
                    if j >= q.ring:
                        h, k = (j - q.ring) // NB, (j - q.ring) % NB
                        if k == NB - 1 and (h + 1) % q.per_group == 0:
                            dve.wait_ge(part_done, (q.group0 + h // q.per_group + 1) * NB)
                        else:
                            dve.wait_ge(prob_used, q.used_count(h, k))
                    nc.vector.scalar_tensor_tensor(mem.prob[0:BP, j % q.ring, :], mem.score[0:BP, j % 3, :], 1.0,
                                                   cnt[0:BP, j % NB, :], ALU.min, ALU.mult).then_inc(prob_ready, 1)

                def tops(j):
                    dve.wait_ge(exp_done, 2 * (P0 + j + 1))
                    t = mem.score[0:BP, j % 3, :]
                    nc.vector.scalar_tensor_tensor(t, t, 1.0, flat[0:BP, j % 2, :], ALU.min, ALU.max
                                                   ).then_inc(top_ready, 1)

                def inverse_sums(i):
                    h, a, width, off = q.groups[i][0]
                    dve.wait_ge(part_done, (q.group0 + i + 1) * NB)
                    if a + width == (h + 1) * q.w:
                        n = q.per_group
                        z = ps[0:BP, 0:NB * 512].rearrange("p (m n) -> p m n", m=NB)[:, :, width - 1::q.w][:, :, 0:n]
                        link(nc.vector.tensor_scalar(mem.z[0:BP, :, 0:n], z, 1e-16, None, ALU.add))
                        link(nc.vector.reciprocal(mem.z[0:BP, :, 0:n], mem.z[0:BP, :, 0:n]))

                def read_group(i, m):
                    for j, (h, a, width, off) in enumerate(q.groups[i]):
                        if a + width == (h + 1) * q.w:
                            width -= 1
                        b0 = a - h * (q.w - q.c)
                        ins = nc.vector.scalar_tensor_tensor(dest(m, a, b0, width), bank(m, off, off + width),
                                                             mem.z[0:BP, m, j:j + 1], bias(m, b0, width),
                                                             ALU.mult, ALU.add)
                    ins.then_inc(part_read, 1)

                for h in range(q.half):
                    head_scores(h)
                for h in range(q.first):
                    for m in range(NB):
                        largest(h, m)
                    columns(h)
                    if h == 0:
                        for other in range(q.half, q.heads):
                            head_scores(other)
                dve.wait_ge(params_loaded, 16 * all_rows)
                tops(0)
                for j in range(q.heads * NB):
                    h, k = j // NB, j % NB
                    if j + 1 < q.heads * NB and k < NB - 1:
                        tops(j + 1)
                    if k == 1 and h and h % q.per_group == 0:
                        inverse_sums(h // q.per_group - 1)
                        for m in range(NB):
                            read_group(h // q.per_group - 1, m)
                    probs(j)
                    if q.first <= h + 2 < q.heads:
                        k0 = 1 if q.stored else 3
                        if k in (k0, k0 + 1):
                            for m in ((0, 1, 2), (3, 4))[k - k0]:
                                largest(h + 2, m)
                        if k == k0 + 1:
                            columns(h + 2)
                    if j + 1 < q.heads * NB and k == NB - 1:
                        tops(j + 1)
                for i in range(q.heads // q.per_group - 1, len(q.groups)):
                    inverse_sums(i)
                    if i < len(q.groups) - 1:
                        for m in range(NB):
                            read_group(i, m)
                            if between is not None:
                                dve.wait_ge(part_read, (q.group0 + i) * NB + m + 1)
                                between(m)
                last = len(q.groups) - 1

                def out(m):
                    read_group(last, m)
                    dve.wait_ge(part_read, (q.group0 + last) * NB + m + 1)

                in_steps((out, 0), *tail)

            def in_place(q):
                return lambda m, a, b0, width: feat_flat(q, m, a, a + width)

            def row_of(t):
                return lambda m, b0, width: t[0:BP, b0:b0 + width]

            def by_heads(row):
                return row[0:BP, 0:HID].rearrange("p (h c) -> p h c", h=HEADS2)

            def q0_stats(m):
                stat(m, 0, feat(Q0, m, 0, 2))
                link(stat(m, 1, feat(Q0, m, 2, 4)))
                var(2, m)

            def q0_out(m):
                t = feat(Q0, m)
                dve.wait_ge(gained, m + 1)
                link(nc.vector.tensor_tensor(t, t, by_heads(mem.par[2]), ALU.add))
                dve.wait_ge(bias_added, m + 1)
                nc.vector.scalar_tensor_tensor(t, t, 0.0, by_heads(mem.resid[:, m, :]), ALU.max, ALU.add
                                               ).then_inc(layer_ready, 1)

            attention(Q0, row_of(mem.par[0]), mem.par[0], mem.par[1], in_place(Q0), 4, 6,
                      [(q0_stats, 0), (shift(2), 1), (q0_out, 3), (lo(T_Q[1], K8), 4)])

            def q1_second(m):
                stat(m, 1, feat_flat(Q1, m, HW, D))

            def q1_stats(m):
                link(stat(m, 0, feat_flat(Q1, m, 0, HW)))
                var(3, m)

            def q1_out(m):
                t = feat_flat(Q1, m, 0, D)
                dve.wait_ge(gained, NB + m + 1)
                dve.wait_ge(bias_added, NB + 3 * (m + 1))
                link(nc.vector.tensor_tensor(t, t, mem.resid[0:BP, m, 0:D], ALU.add))
                stat(m, 0, feat_flat(Q1, m, 0, HW))
                link(stat(m, 1, feat_flat(Q1, m, HW, D)))
                var(4, m)

            attention(Q1, row_of(mem.par[1]), mem.par[0], mem.par0b, in_place(Q1), 10, 12,
                      [(q1_stats, 0), (shift(3), 1), (q1_out, 3), (shift(4), 4), (lo(T_Q[2]), 6)], q1_second)

            def elu(m):
                dve.wait_ge(elu_out, m + 1)
                e, t = mem.feat[0:BP, m * D:(m + 1) * D], mem.resid[0:BP, m, 0:D]
                link(nc.vector.tensor_scalar(e, e, 1.0, -1.0, ALU.min, ALU.add))
                nc.vector.scalar_tensor_tensor(t, t, 0.0, e, ALU.max, ALU.add).then_inc(layer_ready, 1)

            attention(Q2, row_of(mem.par[1]), mem.par[0], mem.par0b,
                      lambda m, a, b0, width: mem.resid[0:BP, m, b0:b0 + width], 15, 15,
                      [(elu, 1), (lo(T_Q[3]), 3)])

            def last_bias(m, b0, width):
                dve.wait_ge(res_biased, m + 1)
                return x_res(m, b0, b0 + width)

            def last_second(m):
                stat(m, 1, x_nat(m, HW))

            def last_stats(m):
                link(stat(m, 0, x_nat(m, 0, HW)))
                var(5, m)

            attention(Q3, last_bias, mem.par[0], mem.par0b,
                      lambda m, a, b0, width: mem.xn[0:BP, m, b0:b0 + width], 18, 18,
                      [(last_stats, 0), (shift(5), 1)], last_second)

        @block.tensor
        def _(pe):

            def of(t):
                return lambda m, c: t[0:BP, m, c * 128:(c + 1) * 128]

            def turn(k, column, u0, m):
                for i in range(2):
                    if 2 * m + i >= 3:
                        pe.wait_ge(xT_lo_ready, u0 + (2 * m + i - 2))
                    b = unit_bank(m, i) * 512
                    for j, (c, _) in enumerate(unit(k, m, i)):
                        ins = nc.tensor.transpose(ps[:, b + j * BP:b + (j + 1) * BP], column(m, c),
                                                  mem.ident[0:BP, 0:BP])
                    ins.then_inc(turned, 1)

            def gemm_block(o, xh, xl, m, k, c, static, width, stop, owed=False):
                for j in range(k):
                    if m == 0:
                        pe.wait_ge(w_lo_ready, c + (j + 1))
                    slot = (static + j) % WRING
                    h, l, wh, wl = xh[:, j, nodes(m)], xl[:, j, nodes(m)], mem.wh[:, slot, 0:width], mem.wl[:, slot, 0:width]
                    ins = nc.tensor.matmul(o, h, wl, start=(j == 0), stop=False, skip_group_check=True)
                    if owed and j == 0:
                        ins.then_inc(w_used, 1)
                    nc.tensor.matmul(o, l, wh, start=False, stop=False, skip_group_check=True)
                    ins = nc.tensor.matmul(o, h, wh, start=False, stop=stop and j == k - 1, skip_group_check=True)
                    if m == NB - 1 and j < k - 1:
                        ins.then_inc(w_used, 1)
                return ins

            def aggregate(adj_h, adj_l, s, slot, i, start, stop, after_gemm, free=None):
                pe.wait_ge(h_lo_ready, i + 1)
                for m in range(NB):
                    if free is not None:
                        pe.wait_ge(out_read, free + m + 1)
                    o, ah, al = bank(m, 0, HW), adj_h[0:BP, s, nodes(m)], adj_l[0:BP, s, nodes(m)]
                    ins = nc.tensor.matmul(o, ah, mem.hl[0:BP, slot, :], start=start, stop=False, skip_group_check=True)
                    if after_gemm and m == 0:
                        ins.then_inc(w_used, 1)
                    nc.tensor.matmul(o, al, mem.hh[0:BP, slot, :], start=False, stop=False, skip_group_check=True)
                    ins = nc.tensor.matmul(o, ah, mem.hh[0:BP, slot, :], start=False, stop=stop, skip_group_check=True)
                    if stop:
                        ins.then_inc(out_done, 1)
                if not stop:
                    ins.then_inc(agg_used, 1)

            def agg1(layer, f, s, after_gemm):
                n = f * NB + s
                if layer == 0 and n == 0:
                    pe.wait_ge(gcn_lo_ready, NB)
                aggregate(mem.ch, mem.cl, s, n % 2, H_L1 + layer * 2 * NB + n, s == 0, s == NB - 1, after_gemm,
                          RLAYERS * 10 + layer * 10 if s == 0 and f else None)

            pe.wait_ge(consts_ready, 2)
            pe.wait_ge(x_loaded, 16)
            for m in range(NB):
                turn(KC, of(mem.xn), 0, m)
            pe.wait_ge(xT_lo_ready, UNITS)

            pe.sem_inc(onehot_used, OH_RING)
            with pe.Fori(0, CHUNKS) as c:
                for p in range(2):
                    def into(j, t):
                        b, a, e = SWEEP_BANKS[j]
                        slot = (p * SWEEP + t) % OH_RING
                        ins = []
                        for m in range(4) if b == 5 else [4] if b == 6 else [b]:
                            o = bank(b, m % 4 * TAIL, m % 4 * TAIL + TAIL) if b >= 5 else bank(b)
                            ins.append(nc.tensor.matmul(o, mem.oh_src[0:BP, slot, nodes(m)],
                                                        mem.oh_dst[0:BP, slot, a:e],
                                                        start=(t == 0) and (b != 5 or m == 0), stop=(t == SWEEP - 1),
                                                        skip_group_check=True))
                        return ins

                    for t in range(SWEEP - LAST_TILES):
                        pe.wait_ge(onehot_ready, c * (2 * SWEEP) + (p * SWEEP + t + 1))
                        for j in range(len(SWEEP_BANKS)):
                            if t == 0:
                                pe.wait_ge(sweep_read, c * 14 + p * (j + 1) + 1)
                            ins = into(j, t)
                            if t == 0 and j == 0 and p:
                                ins[0].then_inc(onehot_used, 1)
                        ins[-1].then_inc(onehot_used, 1)
                    pe.wait_ge(onehot_ready, c * (2 * SWEEP) + (p * SWEEP + SWEEP))
                    for j in range(len(SWEEP_BANKS)):
                        for t in range(SWEEP - LAST_TILES, SWEEP):
                            ins = into(j, t)
                            if t == SWEEP - 1:
                                ins[-1].then_inc(sweep_done, 1)
                            elif j == len(SWEEP_BANKS) - 1:
                                ins[-1].then_inc(onehot_used, 1)
                pe.wait_ge(sweep_done, c * 14 + 14)
                pe.sem_inc(onehot_used, 1)

            pe.wait_ge(sweep_read, 14 * CHUNKS + 1)
            ones = mem.ones[0:BP, 0:1].to_broadcast([BP, BP])
            for m in range(NB):
                pe.wait_ge(decoded, CHUNKS * 40 + 4 * (m + 1) + 1)
                for r in range(NREL):
                    for a, e in ((0, 512), (512, N)):
                        ins = nc.tensor.matmul(ps[0:BP, r * 1024 + a:r * 1024 + e], ones, mem.cnt[0:BP, r, m, a:e],
                                               start=(m == 0), stop=(m == NB - 1))
                    if m == NB - 1:
                        ins.then_inc(degree_done, 1)
            pe.wait_ge(inv_ready, NREL)

            def root(l, f, m):
                static = f * (L0_CHUNKS // 2)
                ins = gemm_block(bank(m, 0, HW), mem.xh, mem.xl, m, KC, l * L0_CHUNKS + static, static, HW, False)
                if m == NB - 1:
                    ins.then_inc(w_used, 1)

            def relations(l, f):
                static = f * (L0_CHUNKS // 2)
                c = l * L0_CHUNKS + static

                def agg(i, after_gemm):
                    r, s = i // NB, i % NB
                    if s == 0:
                        pe.wait_ge(adj_lo_ready, (r + 1) * NB)
                    n = f * (H_LAYER // 2) + i
                    aggregate(mem.ah[:, r], mem.al[:, r], s, n % 2, l * H_LAYER + n, False,
                              i == H_LAYER // 2 - 1, after_gemm)

                for i in range(H_LAYER // 2):
                    r, s = i // NB, i % NB
                    n = f * (H_LAYER // 2) + i
                    if n >= 2:
                        pe.wait_ge(h_lo_ready, l * H_LAYER + (n - 1))
                    k0 = KC * (1 + r)
                    gemm_block(bank(5 + n % 2, 0, HW), mem.xh, mem.xl, s, KC, c + k0, static + k0, HW, True
                               ).then_inc(h_done, 1)
                    if i:
                        agg(i - 1, s == NB - 1)
                agg(H_LAYER // 2 - 1, False)

            def relational(l):
                relations(l, 0)
                for m in range(NB):
                    pe.wait_ge(out_read, l * 10 + (m + 1))
                    root(l, 1, m)
                relations(l, 1)

            for m in range(NB):
                root(0, 0, m)
            with pe.Fori(0, RLAYERS - 1) as l:
                relational(l)

                def turn_out(m):
                    pe.wait_ge(out_read, l * 10 + (NB + m + 1))
                    turn(KC, of(mem.xn), l * UNITS + UNITS, m)

                def next_root(m):
                    pe.wait_ge(xT_lo_ready, l * UNITS + (UNITS + 2 * (m + 1)))
                    root(l + 1, 0, m)

                in_steps((turn_out, 0), (next_root, 2))
            relational(RLAYERS - 1)

            def turn_normed(n, u0):
                def stage(m):
                    pe.wait_ge(normed[n], m + 1)
                    turn(KC, of(mem.xres), u0, m)
                return stage

            def degree(m):
                if m == 0:
                    pe.wait_ge(loops_added, NB)
                    pe.wait_ge(out_read, RLAYERS * 10 - NB + 1)
                for s in range(NB):
                    ins = nc.tensor.matmul(bank(0, m, m + 1), mem.cf[0:BP, s, nodes(m)], mem.ones[0:BP, 0:1],
                                           start=(s == 0), stop=(s == NB - 1))
                if m == NB - 1:
                    ins.then_inc(gdeg_done, 1)

            in_steps((degree, 0), (turn_normed(0, T_L1 - UNITS), 1))
            pe.wait_ge(xT_lo_ready, T_L1)

            def mask_row(n):
                m, half = n // 2, n % 2
                if n:
                    pe.wait_ge(mask_read, n)
                a, e = MASK_HALVES[half]
                for s in range(a // BP, e // BP):
                    ins = nc.tensor.matmul(bank(7, s * BP - a, s * BP - a + BP), mem.cf[0:BP, s, nodes(m)],
                                           mem.ident[0:BP, 0:BP], start=True, stop=True)
                ins.then_inc(mask_done, 1)

            for layer in range(2):
                if layer:
                    for m in range(NB):
                        pe.wait_ge(out_read, RLAYERS * 10 + NB + m + 1)
                        turn(KC, of(mem.xn), T_L1, m)
                for f in range(2):
                    c = BASE_L1 + (layer * 2 + f) * KC
                    for s in range(NB):
                        n = f * NB + s
                        if n >= 2:
                            pe.wait_ge(h_lo_ready, H_L1 + layer * 2 * NB + n - 1)
                        elif layer:
                            pe.wait_ge(xT_lo_ready, T_L1 + UNITS)
                        if layer == 0:
                            mask_row(n)
                        gemm_block(bank(5 + n % 2, 0, HW), mem.xh, mem.xl, s, KC, c, c, HW, True).then_inc(h_done, 1)
                        if s:
                            agg1(layer, f, s - 1, s == NB - 1)
                    agg1(layer, f, NB - 1, False)

            def attention(q, xh, xl, u0, turn_block):
                n = len(q.pieces)
                owed = [False]

                def first_piece(m):
                    pe.wait_ge(xT_lo_ready, u0 + 2 * (m + 1))
                    gemm_block(bank(q.banks[m], 0, q.pieces[0][1]), xh, xl, m, q.k, q.chunk, q.chunk,
                               q.pieces[0][1], True).then_inc(gemm_done, 1)

                def chunk_step(piece, j):
                    c = q.chunk + piece * q.k + j
                    slot, width = c % WRING, q.pieces[piece % n][1]
                    pe.wait_ge(w_lo_ready, c + 1)
                    wh, wl = mem.wh[:, slot, 0:width], mem.wl[:, slot, 0:width]
                    for m in range(NB):
                        g = piece * NB + m
                        if j == 0 and q.free_count(g):
                            pe.wait_ge(gemm_read, q.free_count(g))
                        o, h, l = bank(q.banks[g], 0, width), xh[:, j, nodes(m)], xl[:, j, nodes(m)]
                        ins = nc.tensor.matmul(o, h, wl, start=(j == 0), stop=False, skip_group_check=True)
                        if owed[0]:
                            ins.then_inc(w_used, 1)
                            owed[0] = False
                        nc.tensor.matmul(o, l, wh, start=False, stop=False, skip_group_check=True)
                        ins = nc.tensor.matmul(o, h, wh, start=False, stop=(j == q.k - 1), skip_group_check=True)
                        if j == q.k - 1:
                            ins.then_inc(gemm_done, 1)
                        elif m == NB - 1:
                            ins.then_inc(w_used, 1)
                    if j == q.k - 1:
                        owed[0] = True

                def broadcast_row(t, h, off):
                    for m, p, e, a, z in score_pieces(off):
                        ins = nc.tensor.matmul(ps[0:BP, p:e], t[0:BP, m, h:h + 1].to_broadcast([BP, BP]),
                                               mem.ident[0:BP, a:z], start=True, stop=True)
                        if owed[0] and m == 0:
                            ins.then_inc(w_used, 1)
                            owed[0] = False
                    return ins

                def max_row(h):
                    pe.wait_ge(al_ready, q.al0 + (h + 1) * q.al_head)
                    if h:
                        pe.wait_ge(rows_read, q.head0 + h)
                    elif q.index == 2:
                        pe.wait_ge(gemm_read, q.gemm0 + NB)
                    else:
                        pe.wait_ge(gemm_read, q.gemm0 + NB * n)
                    if h == 1:
                        pe.wait_ge(gemm_read, q.gemm0 + NB * n)
                    broadcast_row(mem.al_src, h, q.rows_col(h)).then_inc(max_row_done, 1)

                def rows_of(h):
                    if q.stored and h:
                        pe.wait_ge(rows_read, q.head0 + h)
                    pe.wait_ge(cols_ready, q.head0 + h + 1)
                    broadcast_row(mem.row1, h, q.rows_col(h))
                    broadcast_row(mem.row2, h, q.rows_col(h) + N).then_inc(rows_done, 1)

                in_steps((turn_block, 0), (first_piece, 2))
                owed[0] = True
                for step in range((len(q.banks) // NB - 1) * q.k):
                    if step in q.max_at:
                        max_row(q.max_at[step])
                    if step in q.rows_at:
                        rows_of(q.rows_at[step])
                    chunk_step(1 + step // q.k, step % q.k)
                for h in range(q.first):
                    if h not in q.max_at.values():
                        max_row(h)
                    if h == 0 and h not in q.rows_at.values():
                        rows_of(h)
                pe.wait_ge(gemm_read, q.gemm0 + len(q.banks))
                if q.stored:
                    pe.wait_ge(rows_read, q.head0 + 1)
                    for h in range(q.first, q.heads):
                        pe.wait_ge(al_ready, q.al0 + (h + 1) * q.al_head)
                        if h >= q.first + 2:
                            pe.wait_ge(al_row_stored, h - q.first - 1)
                        broadcast_row(mem.al_src, h, h % 2 * 1024).then_inc(al_row_done, 1)
                    pe.wait_ge(al_row_stored, q.heads - q.first)

                def sum_block(group, h, a, width, off, k, used):
                    j = h * NB + k
                    last = k == NB - 1 and (h, a, width, off) == q.groups[group][-1]
                    for m in range(NB):
                        if k == 0 and off == 0 and group:
                            pe.wait_ge(part_read, (q.group0 + group - 1) * NB + m + 1)
                        ins = nc.tensor.matmul(bank(m, off, off + width), mem.prob[0:BP, j % q.ring, nodes(m)],
                                               feat_flat(q, k, a, a + width), start=(k == 0 and off == 0),
                                               stop=(k == NB - 1), skip_group_check=True)
                        if owed[0]:
                            ins.then_inc(w_used, 1)
                            owed[0] = False
                        elif last:
                            ins.then_inc(part_done, 1)
                    if used and not last:
                        ins.then_inc(prob_used, 1)

                for h in range(q.heads):
                    group = h // q.per_group
                    if h + 1 < q.heads and h + 1 not in q.rows_at.values() and (h == 0 or not q.stored):
                        rows_of(h + 1)
                    for k in range(NB):
                        if k == 3 and q.first <= h + 2 < q.heads:
                            if q.stored:
                                rows_of(h + 2)
                            else:
                                max_row(h + 2)
                        pe.wait_ge(prob_ready, (q.head0 + h) * NB + k + 1)
                        sum_block(group, *q.groups[group][h % q.per_group], k, q.heads > 1)
                if q.heads == 1:
                    for k in range(NB):
                        sum_block(1, *q.groups[1][0], k, False)

            attention(Q0, mem.xh, mem.xl, T_Q[0], turn_normed(1, T_Q[0]))

            def turn_q0(m):
                pe.wait_ge(layer_ready, m + 1)
                turn(K8, lambda m, c: feat_flat(Q0, m, c // 2 * Q0.w + c % 2 * 128,
                                                c // 2 * Q0.w + c % 2 * 128 + 128), T_Q[1], m)

            attention(Q1, mem.xh8, mem.xl8, T_Q[1], turn_q0)
            attention(Q2, mem.xh, mem.xl, T_Q[2], turn_normed(4, T_Q[2]))

            def turn_q2(m):
                pe.wait_ge(layer_ready, NB + m + 1)
                turn(KC, of(mem.resid), T_Q[3], m)

            attention(Q3, mem.xh, mem.xl, T_Q[3], turn_q2)


def lay_chunks(mats):
    import numpy as np
    out = []
    for w, pieces in mats:
        for a, width in pieces:
            for k in range(w.shape[0] // 128):
                c = np.zeros((128, HW), w.dtype)
                c[:, :width] = w[k * 128:(k + 1) * 128, a:a + width]
                out.append(c)
    return out


def weight_stream(i):
    import numpy as np
    chunks = []
    for layer in "123":
        w, root = i["L0_gnn_W" + layer], i["L0_gnn_root" + layer]
        for piece in PIECES:
            for m in [root] + [w[r] for r in range(NREL)]:
                chunks += lay_chunks([(m, [piece])])
    for n in ("L1_gnn_W1", "L1_gnn_W2"):
        chunks += lay_chunks([(i[n], PIECES)])
    for n in ("L2_gnn_W1", "L2_gnn_Wr1"):
        chunks += lay_chunks([(i[n], PIECES1)])
    for n in ("L2_gnn_W2", "L2_gnn_Wr2"):
        chunks += lay_chunks([(i[n], PIECES)])
    for n in ("L3_gnn_W1", "L3_gnn_W2"):
        chunks += lay_chunks([(i[n], PIECES)])
    return np.ascontiguousarray(np.stack(chunks))


VECTORS = ["L2_gnn_a_src1", "L2_gnn_a_dst1", "L2_gnn_b1", "L2_gnn_g1", "L2_gnn_be1", "L2_gnn_br1",
           "L2_gnn_a_src2", "L2_gnn_a_dst2", "L2_gnn_b2", "L2_gnn_g2", "L2_gnn_be2", "L2_gnn_br2",
           "L3_gnn_a_src1", "L3_gnn_a_dst1", "L3_gnn_b1", "L3_gnn_a_src2", "L3_gnn_a_dst2", "L3_gnn_b2"]


def kernel(**inputs):
    import numpy as np
    import concourse.bacc as bacc
    from concourse.bass_utils import run_bass_kernel_spmd as run
    i = {name: np.asarray(a) for name, a in inputs.items()}
    arrays = {
        "x_dram": i["x"], "src_dram": i["src"], "dst_dram": i["dst"], "edge_type_dram": i["edge_type_4"],
        "weights_dram": weight_stream(i),
        "rgcn_bias_dram": np.stack([i["L0_gnn_b" + layer] for layer in "123"]),
        "gcn_bias_dram": np.stack([i["L1_gnn_b1"], i["L1_gnn_b2"]]),
    }
    for name in VECTORS:
        arrays[name + "_dram"] = i[name].reshape(-1)
    arrays = {name: np.ascontiguousarray(a) for name, a in arrays.items()}
    nc = bacc.Bacc("TRN2", target_bir_lowering=False, num_devices=1)
    aps = [nc.dram_tensor(name, a.shape, mybir.dt.from_np(a.dtype), kind="ExternalInput").ap()
           for name, a in arrays.items()]
    out = nc.dram_tensor("out_dram", (N, D), F32, kind="ExternalOutput").ap()
    program(nc, *aps[:7], dict(zip(VECTORS, aps[7:])), out)
    r = run(nc, [arrays], core_ids=[0])
    return r.results[0]["out_dram"]
```
